# Optimizing a Trainium2 kernel written in Bass

```python
import numpy as np
import jax
import jax.numpy as jnp

def _softmax(x, axis=-1):
    return jax.nn.softmax(x, axis=axis)

def _gelu(x):
    return jax.nn.gelu(x, approximate=True)

def _silu(x):
    return jax.nn.silu(x)

def _sigmoid(x):
    return jax.nn.sigmoid(x)

def _layernorm(x, axis=-1, eps=1e-05):
    m = jnp.mean(x, axis=axis, keepdims=True)
    v = jnp.var(x, axis=axis, keepdims=True)
    return (x - m) / jnp.sqrt(v + eps)

def _scatter_add(tgt, idx, src, axis=0):
    return tgt.at[idx].add(src)

def _segment_sum(src, seg, n):
    return jax.ops.segment_sum(src, seg, n)
kernel_name = 'mk_gnn_resnorm_d2_gnn_r8_c75069'

def setup_inputs(seed: int=0):
    np.random.seed(seed)
    _w = jnp.asarray

    def _rec_inputs():
        import jax
        import jax.numpy as jnp
        _gk = jax.random.key(seed)
        x = -0.000202 + 1 * jax.random.normal(jax.random.fold_in(_gk, 1), (6250, 128), jnp.float32)
        src = jax.random.randint(jax.random.fold_in(_gk, 2), (100000,), 0, 6250, jnp.int32)
        dst = jax.random.randint(jax.random.fold_in(_gk, 3), (100000,), 0, 6250, jnp.int32)
        _o = jnp.argsort(dst, stable=True)
        src = src[_o]
        dst = dst[_o]
        edge_weight = jax.random.uniform(jax.random.fold_in(_gk, 13), (100000,), jnp.float32, 0.0, 1)
        return (x, src, dst, edge_weight)
    x, src, dst, edge_weight = _rec_inputs()

    def _L0_gnn_setup():
        import jax, jax.numpy as jnp
        import numpy as np
        N_NODES = 6250
        N_EDGES = 100000
        NODE_DIM = 128
        HIDDEN = 256

        def _glorot(key, shape):
            fan_in, fan_out = (shape[0], shape[1])
            lim = np.sqrt(6.0 / (fan_in + fan_out)).astype(np.float32)
            return jax.random.uniform(key, shape, jnp.float32, -lim, lim)
        key = jax.random.key(seed)
        ks = jax.random.split(key, 12)
        node_features = jax.random.normal(ks[0], (N_NODES, NODE_DIM), jnp.float32)
        edge_index = jax.random.randint(ks[1], (2, N_EDGES), 0, N_NODES, jnp.int64)
        return {'node_features': node_features, 'edge_index': edge_index, 'Wm1': _glorot(ks[2], (2 * NODE_DIM, HIDDEN)), 'bm1': jnp.zeros((HIDDEN,), jnp.float32), 'Wm2': _glorot(ks[3], (HIDDEN, HIDDEN)), 'bm2': jnp.zeros((HIDDEN,), jnp.float32), 'Wm3': _glorot(ks[4], (HIDDEN, NODE_DIM)), 'bm3': jnp.zeros((NODE_DIM,), jnp.float32), 'Wn1': _glorot(ks[5], (2 * NODE_DIM, HIDDEN)), 'bn1': jnp.zeros((HIDDEN,), jnp.float32), 'Wn2': _glorot(ks[6], (HIDDEN, NODE_DIM)), 'bn2': jnp.zeros((NODE_DIM,), jnp.float32)}
    _L0_gnn_all = _L0_gnn_setup()
    _L0_gnn_in = {k: v for k, v in _L0_gnn_all.items() if k in ('Wm1', 'bm1', 'Wm2', 'bm2', 'Wm3', 'bm3', 'Wn1', 'bn1', 'Wn2', 'bn2')}
    del _L0_gnn_all

    def _L1_gnn_setup():
        import jax, jax.numpy as jnp
        import numpy as np
        N_NODES = 6250
        N_EDGES = 100000
        HID = 128
        key = jax.random.key(seed)
        ks = jax.random.split(key, 10)
        s_msg = 1.0 / np.sqrt(2 * HID + 1)
        s_u1 = 1.0 / np.sqrt(2 * HID)
        s_u2 = 1.0 / np.sqrt(HID)
        return {'z': jax.random.normal(ks[0], (N_NODES, HID), dtype=jnp.float32), 'edge_weight': jax.random.uniform(ks[1], (N_EDGES,), dtype=jnp.float32), 'edge_src': jax.random.randint(ks[2], (N_EDGES,), 0, N_NODES), 'edge_dst': jax.random.randint(ks[3], (N_EDGES,), 0, N_NODES), 'Wm': jax.random.normal(ks[4], (2 * HID + 1, HID), dtype=jnp.float32) * s_msg, 'bm': jax.random.normal(ks[5], (HID,), dtype=jnp.float32) * s_msg, 'W1': jax.random.normal(ks[6], (2 * HID, HID), dtype=jnp.float32) * s_u1, 'b1': jax.random.normal(ks[7], (HID,), dtype=jnp.float32) * s_u1, 'W2': jax.random.normal(ks[8], (HID, HID), dtype=jnp.float32) * s_u2, 'b2': jax.random.normal(ks[9], (HID,), dtype=jnp.float32) * s_u2}
    _L1_gnn_all = _L1_gnn_setup()
    _L1_gnn_in = {k: v for k, v in _L1_gnn_all.items() if k in ('Wm', 'bm', 'W1', 'b1', 'W2', 'b2')}
    del _L1_gnn_all
    return {'x': x, 'src': src, 'dst': dst, 'edge_weight': edge_weight, 'L0_gnn_Wm1': _L0_gnn_in['Wm1'], 'L0_gnn_bm1': _L0_gnn_in['bm1'], 'L0_gnn_Wm2': _L0_gnn_in['Wm2'], 'L0_gnn_bm2': _L0_gnn_in['bm2'], 'L0_gnn_Wm3': _L0_gnn_in['Wm3'], 'L0_gnn_bm3': _L0_gnn_in['bm3'], 'L0_gnn_Wn1': _L0_gnn_in['Wn1'], 'L0_gnn_bn1': _L0_gnn_in['bn1'], 'L0_gnn_Wn2': _L0_gnn_in['Wn2'], 'L0_gnn_bn2': _L0_gnn_in['bn2'], 'L1_gnn_Wm': _L1_gnn_in['Wm'], 'L1_gnn_bm': _L1_gnn_in['bm'], 'L1_gnn_W1': _L1_gnn_in['W1'], 'L1_gnn_b1': _L1_gnn_in['b1'], 'L1_gnn_W2': _L1_gnn_in['W2'], 'L1_gnn_b2': _L1_gnn_in['b2']}

def reference(x, src, dst, edge_weight, L0_gnn_Wm1, L0_gnn_bm1, L0_gnn_Wm2, L0_gnn_bm2, L0_gnn_Wm3, L0_gnn_bm3, L0_gnn_Wn1, L0_gnn_bn1, L0_gnn_Wn2, L0_gnn_bn2, L1_gnn_Wm, L1_gnn_bm, L1_gnn_W1, L1_gnn_b1, L1_gnn_W2, L1_gnn_b2):
    import jax
    import jax.numpy as jnp

    def _L0_gnn_ref(node_features, edge_index, Wm1, bm1, Wm2, bm2, Wm3, bm3, Wn1, bn1, Wn2, bn2):
        import jax, jax.numpy as jnp
        import numpy as np
        N_NODES = 6250
        N_EDGES = 100000
        NODE_DIM = 128
        HIDDEN = 256

        def _glorot(key, shape):
            fan_in, fan_out = (shape[0], shape[1])
            lim = np.sqrt(6.0 / (fan_in + fan_out)).astype(np.float32)
            return jax.random.uniform(key, shape, jnp.float32, -lim, lim)
        num_nodes = node_features.shape[0]
        row, col = (edge_index[0], edge_index[1])
        msg_in = jnp.concatenate([node_features[row], node_features[col]], axis=-1)
        h = jax.nn.relu(msg_in @ Wm1 + bm1)
        h = jax.nn.relu(h @ Wm2 + bm2)
        messages = h @ Wm3 + bm3
        agg = jax.ops.segment_sum(messages, col, num_segments=num_nodes)
        count = jax.ops.segment_sum(jnp.ones((messages.shape[0],), messages.dtype), col, num_segments=num_nodes)
        agg = agg / jnp.clip(count, 1.0)[:, None]
        node_in = jnp.concatenate([node_features, agg], axis=-1)
        upd = jax.nn.relu(node_in @ Wn1 + bn1) @ Wn2 + bn2
        return node_features + upd

    def _L1_gnn_ref(z, edge_weight, edge_src, edge_dst, Wm, bm, W1, b1, W2, b2):
        import jax, jax.numpy as jnp
        import numpy as np
        N_NODES = 6250
        N_EDGES = 100000
        HID = 128
        n, H = z.shape
        Wd, Ws, ww = (Wm[:H], Wm[H:2 * H], Wm[2 * H])
        msgs = z[edge_dst] @ Wd + z[edge_src] @ Ws + edge_weight[:, None] * ww[None, :] + bm
        agg = jax.ops.segment_max(msgs, edge_dst, num_segments=n)
        deg = jax.ops.segment_sum(jnp.ones_like(edge_weight), edge_dst, num_segments=n)
        agg = jnp.where(deg[:, None] > 0, agg, jnp.zeros((), dtype=z.dtype))
        W1a, W1b = (W1[:H], W1[H:])
        hidden = jax.nn.relu(z @ W1a + agg @ W1b + b1)
        return hidden @ W2 + b2
    edge_index = jnp.stack([src, dst])
    x = _layernorm(x + _L0_gnn_ref(x, edge_index, L0_gnn_Wm1, L0_gnn_bm1, L0_gnn_Wm2, L0_gnn_bm2, L0_gnn_Wm3, L0_gnn_bm3, L0_gnn_Wn1, L0_gnn_bn1, L0_gnn_Wn2, L0_gnn_bn2), axis=-1)
    x = _layernorm(x + _L1_gnn_ref(x, edge_weight, src, dst, L1_gnn_Wm, L1_gnn_bm, L1_gnn_W1, L1_gnn_b1, L1_gnn_W2, L1_gnn_b2), axis=-1)
    return x

_drawn_inputs = setup_inputs


def setup_inputs(seed=0):
    import zlib

    import numpy as np

    out = dict(_drawn_inputs(seed))
    spreads = {'L0_gnn_bm1': (0.0, 0.8),
     'L0_gnn_bm2': (0.0, 0.414),
     'L0_gnn_bm3': (0.0, 0.41),
     'L0_gnn_bn1': (0.0, 0.1),
     'L0_gnn_bn2': (0.0, 0.1)}
    factors = {'edge_weight': 8.0}
    for name, (base, spread) in spreads.items():
        noise = np.random.default_rng([zlib.crc32(name.encode()), seed]).standard_normal(out[name].shape)
        drawn = base * np.exp(spread * noise) if base else spread * noise
        out[name] = jnp.asarray(drawn.astype(out[name].dtype))
    for name, factor in factors.items():
        out[name] = (out[name] * factor).astype(out[name].dtype)
    return out
```

```python
from contextlib import ExitStack

import numpy as np

import concourse.bass as bass
from concourse import mybir
from concourse.alu_op_type import AluOpType as ALU

F32 = mybir.dt.float32
BF16 = mybir.dt.bfloat16
I32 = mybir.dt.int32
ACT = mybir.ActivationFunctionType

N, E, D, H = 6250, 100000, 128, 256
P = 128
T = 512
G = T // P
U = 4
IT = -(-E // (T * U))
TILES = IT * U
EP = TILES * T
ROWS = EP // P
NB = -(-N // P)
NB += NB % 2
NP = NB * P
FAR = float(NP)
RESTART = -3.0e38
EPS = 1e-5


def at_least(eng, sem, value):
    if isinstance(value, int) and value <= 0:
        return
    eng.wait_ge(sem, value)


def over(eng, body, count):
    body(0)
    with eng.Fori(1, count - 1) as i:
        body(i)
    body(count - 1)


def staged(eng, body, stages):
    lead = (stages + 3) // 2
    pairs = (NB + stages - 1 + 1) // 2
    full = NB // 2

    def pair(j, fixed):
        for u in range(2):
            k = 2 * j + u
            live = [not fixed or 0 <= k - s < NB for s in range(stages)]
            if any(live):
                body(k, u, live)

    for j in range(lead):
        pair(j, True)
    with eng.Fori(lead, full) as j:
        pair(j, False)
    for j in range(full, pairs):
        pair(j, True)


def col(t, i):
    return t[:, bass.ds(i, 1)] if not isinstance(i, int) else t[:, i:i + 1]


def rows(t, i, n=P):
    return t[n * i:n * i + n, :] if isinstance(i, int) else t[bass.ds(i * n, n), :]


def program(nc, d):
    ctx = ExitStack()
    with ctx:
        def sb(name, shape, dt=F32):
            return ctx.enter_context(nc.sbuf_tensor(name, shape, dt))

        def sem(name):
            return ctx.enter_context(nc.semaphore(name))

        def dram(name, shape, dt=F32):
            return nc.dram_tensor(name, shape, dt, kind="Internal").ap()

        a_t, b_t = dram("a_t", (NP, H)), dram("b_t", (NP, H))
        keep_t, pen_t = dram("keep_t", (EP,), BF16), dram("pen_t", (EP,), BF16)
        sum_t = dram("sum_t", (EP, H))
        z_t, p_t = dram("z_t", (NP, D)), dram("p_t", (NP, D))
        max_t = dram("max_t", (EP, D))

        diag = sb("diag", [P, 2 * P])
        ident = diag[:, 1:P + 1]
        below = diag[:, 0:P]
        wrap = diag[:, P:2 * P]
        wm1 = sb("wm1", [P, 2 * H])
        wm2 = sb("wm2", [P, 2, H])
        wm3 = sb("wm3", [P, 2, D])
        wn1 = sb("wn1", [P, 2, H])
        wn2 = sb("wn2", [P, 2, D])
        wd_s = sb("wd_s", [P, 2, D])
        ww = sb("ww", [1, D])
        w1 = sb("w1", [P, 2, D])
        w2 = sb("w2", [P, D])
        ab_bias = sb("ab_bias", [P, 2 * H])
        bm2 = sb("bm2", [P, 2])
        bn1 = sb("bn1", [P, 2])
        b1 = sb("b1", [P, 1])
        bm3 = sb("bm3", [P, D])
        bn2 = sb("bn2", [P, D])
        bm = sb("bm", [P, D])
        b2 = sb("b2", [P, D])
        eps = sb("eps", [P, 1])
        node = sb("node", [P, NB])
        node_i = sb("node_i", [P, NB], I32)
        src = sb("src", [P, ROWS], I32)
        dst = sb("dst", [P, ROWS], I32)
        cnt = sb("cnt", [P, NB + 1])
        tiles_le = sb("tiles_le", [P, NB])
        fine = sb("fine", [P, NB])
        rcp = sb("rcp", [P, NB])
        flag = sb("flag", [P, NB])
        end_f = sb("end_f", [P, NB])
        idx = sb("idx", [P, 2], I32)

        s_turn, s_aggr = sem("pool_turn"), sem("dve_aggr")

        bank = [ctx.enter_context(nc.psum_tensor(f"bank{i}", [P, 512], F32)) for i in range(8)]

        with ExitStack() as sx:
            def tmp(name, shape, dt=F32):
                return sx.enter_context(nc.sbuf_tensor(name, shape, dt))
            W = EP // P
            cur_i, prev_i = tmp("cur_i", [P, W], I32), tmp("prev_i", [P, W], I32)
            cur, prev = tmp("cur", [P, W]), tmp("prev", [P, W])
            keep, pen = tmp("keep", [P, W], BF16), tmp("pen", [P, W], BF16)
            last_i, last = tmp("last_i", [P, ROWS], I32), tmp("last", [P, ROWS])
            hit = tmp("hit", [P, ROWS])
            row_i = tmp("row_i", [P, 2, P], I32)
            row_f, row_hit = tmp("row_f", [P, P]), tmp("row_hit", [P, P])
            s_diag, s_w, s_edges, s_iota = sem("s_diag"), sem("s_w"), sem("s_edges"), sem("s_iota")
            s_mask, s_mask_st = sem("s_mask"), sem("s_mask_st")
            s_cast, s_coarse, s_idx = sem("s_cast"), sem("s_coarse"), sem("s_idx")
            s_row = [sem("s_row0"), sem("s_row1")]
            s_rowf, s_hit, s_cnt, s_deg_ps, s_deg = sem("s_rowf"), sem("s_hit"), sem("s_cnt"), sem("s_deg_ps"), sem("s_deg")
            s_zero = sem("s_zero")
            block = sx.enter_context(nc.Block())

            @block.sync
            def _(sp):
                sp.dma_start(cur_i[:, :], d["dst_cur"].rearrange("(p c) -> p c", p=P)).then_inc(s_edges, 16)
                sp.dma_start(prev_i[:, :], d["dst_prev"].rearrange("(p c) -> p c", p=P)).then_inc(s_edges, 16)
                sp.dma_start(last_i[:, :], d["dst_last"].partition_broadcast(P)).then_inc(s_edges, 16)
                sp.dma_start(src[:, :], d["src"]).then_inc(s_edges, 16)
                sp.dma_start(dst[:, :], d["dst"]).then_inc(s_edges, 16)
                halves = {"L0_gnn_Wm1": wm1.rearrange("p (a n) -> p a n", a=2), "L0_gnn_Wm2": wm2, "L0_gnn_Wm3": wm3,
                          "L0_gnn_Wn1": wn1, "L0_gnn_Wn2": wn2, "L1_gnn_W1": w1}
                for name, t in halves.items():
                    sp.dma_start(t[:, :, :], d[name].rearrange("(a p) n -> p a n", p=P)).then_inc(s_w, 16)
                sp.dma_start(wd_s[:, :, :], d["L1_gnn_Wm"][0:2 * D, :].rearrange("(a p) n -> p a n", p=P)).then_inc(s_w, 16)
                sp.dma_start(ww[:, :], d["L1_gnn_Wm"][2 * D:2 * D + 1, :]).then_inc(s_w, 16)
                sp.dma_start(w2[:, :], d["L1_gnn_W2"]).then_inc(s_w, 16)
                sp.dma_start(ab_bias[:, H:2 * H], d["L0_gnn_bm1"].partition_broadcast(P)).then_inc(s_w, 16)
                for name, t in {"L0_gnn_bm3": bm3, "L0_gnn_bn2": bn2, "L1_gnn_bm": bm, "L1_gnn_b2": b2}.items():
                    sp.dma_start(t[:, :], d[name].partition_broadcast(P)).then_inc(s_w, 16)
                for name, t in {"L0_gnn_bm2": bm2, "L0_gnn_bn1": bn1, "L1_gnn_b1": b1}.items():
                    sp.dma_start(t[:, :], d[name]).then_inc(s_w, 16)
                sp.wait_ge(s_mask, 2)
                sp.dma_start(keep_t.rearrange("(p c) -> p c", p=P), keep[:, :]).then_inc(s_mask_st, 16)
                sp.dma_start(pen_t.rearrange("(p c) -> p c", p=P), pen[:, :]).then_inc(s_mask_st, 16)
                sp.wait_ge(s_mask_st, 32)
                sp.wait_ge(s_edges, 5 * 16)
                sp.wait_ge(s_w, 17 * 16)

            @block.gpsimd
            def _(pool):
                pool.memset(diag[:, :], 0.0).then_inc(s_diag, 1)
                pool.wait_ge(s_diag, 1)
                pool.affine_select(out=diag[:, :], in_=diag[:, :], compare_op=ALU.not_equal, fill=1.0, base=1,
                                   pattern=[[-1, 2 * P]], channel_multiplier=1).then_inc(s_diag, 1)
                pool.iota(node_i[:, :], pattern=[[P, NB]], base=0, channel_multiplier=1).then_inc(s_iota, 1)

                def fetch_row(b, q):
                    pool.wait_ge(s_idx, b + 1)
                    pool.sem_inc(s_turn, 1)
                    pool.indirect_dma_start(row_i[:, q, :], None, d["dst_rows"],
                                            bass.IndirectOffsetOnAxis(ap=idx[:, q:q + 1], axis=0)).then_inc(s_row[q], 16)
                staged(pool, lambda k, u, live: fetch_row(k, u), 1)

            @block.vector
            def _(dve):
                dve.memset(eps[:, :], EPS)
                dve.memset(ab_bias[:, 0:H], 0.0)
                dve.memset(cnt[:, 0:1], 0.0).then_inc(s_zero, 1)
                dve.wait_ge(s_edges, 5 * 16)
                dve.tensor_copy(cur[:, :], cur_i[:, :])
                dve.tensor_copy(prev[:, :], prev_i[:, :])
                dve.tensor_copy(last[:, :], last_i[:, :])
                dve.wait_ge(s_iota, 1)
                dve.tensor_copy(node[:, :], node_i[:, :]).then_inc(s_cast, 1)
                dve.wait_ge(s_cast, 1)
                dve.tensor_tensor(keep[:, :], cur[:, :], prev[:, :], ALU.is_equal).then_inc(s_mask, 1)
                dve.wait_ge(s_mask, 1)
                dve.tensor_scalar(pen[:, :], keep[:, :], -RESTART, RESTART, ALU.mult, ALU.add).then_inc(s_mask, 1)

                def count(k, u, live):
                    if live[2]:
                        b = k - 2
                        dve.wait_ge(s_row[u], (k - u) * 8 if not isinstance(k, int) else 16 * (k // 2))
                        at_least(dve, s_hit, b)
                        dve.tensor_copy(row_f[:, :], row_i[:, u, :]).then_inc(s_rowf, 1)
                        dve.wait_ge(s_rowf, b + 1)
                        dve.tensor_scalar(row_hit[:, :], row_f[:, :], col(node, b), 0.0, ALU.is_le, ALU.add,
                                          accum_out=col(fine, b)).then_inc(s_hit, 1)
                    if live[0]:
                        at_least(dve, s_coarse, k)
                        dve.tensor_scalar(hit[:, :], last[:, :], col(node, k), 0.0, ALU.is_le, ALU.add,
                                          accum_out=col(tiles_le, k)).then_inc(s_coarse, 1)
                        dve.wait_ge(s_coarse, k + 1)
                        dve.tensor_scalar(idx[:, u:u + 1], col(tiles_le, k), 1.0, None, ALU.mult).then_inc(s_idx, 1)
                staged(dve, count, 3)
                dve.wait_ge(s_hit, NB)
                dve.wait_ge(s_coarse, NB)
                dve.scalar_tensor_tensor(cnt[:, 1:NB + 1], tiles_le[:, :], float(P), fine[:, :],
                                         ALU.mult, ALU.add).then_inc(s_cnt, 1)
                dve.wait_ge(s_cnt, 1)
                dve.tensor_scalar(end_f[:, :], cnt[:, 1:NB + 1], 1.0, 0.0, ALU.subtract, ALU.max).then_inc(s_cnt, 1)
                dve.wait_ge(s_deg_ps, 1)
                dve.tensor_tensor(fine[:, :], cnt[:, 1:NB + 1], bank[0][:, 0:NB], ALU.subtract).then_inc(s_deg, 1)
                dve.wait_ge(s_deg, 1)
                dve.tensor_scalar(flag[:, :], fine[:, :], 1.0, None, ALU.min).then_inc(s_deg, 1)
                dve.tensor_scalar(tiles_le[:, :], fine[:, :], 1.0, None, ALU.max).then_inc(s_deg, 1)
                dve.wait_ge(s_deg, 3)
                dve.reciprocal(rcp[:, :], tiles_le[:, :]).then_inc(s_deg, 1)

            @block.tensor
            def _(pe):
                pe.wait_ge(s_diag, 2)
                pe.wait_ge(s_cnt, 1)
                pe.wait_ge(s_zero, 1)
                pe.matmul(bank[0][:, 0:NB], below, cnt[:, 1:NB + 1], start=True, stop=False)
                pe.matmul(bank[0][:, 0:NB], wrap, cnt[:, 0:NB], start=False, stop=True).then_inc(s_deg_ps, 1)

        with ExitStack() as sx:
            def tmp(name, shape, dt=F32):
                return sx.enter_context(nc.sbuf_tensor(name, shape, dt))
            xb, xt, ab = tmp("xb", [P, 2, D]), tmp("xt", [P, 2, P]), tmp("ab", [P, 2, 2 * H])
            s_x = [sem("s_x0"), sem("s_x1")]
            s_st = [sem("s_ab0"), sem("s_ab1")]
            s_xt_ps, s_xt, s_ab_ps, s_ab = sem("s_xt_ps"), sem("s_xt"), sem("s_ab_ps"), sem("s_ab")
            block = sx.enter_context(nc.Block())

            @block.sync
            def _(sp):
                def step(k, u, live):
                    if live[0]:
                        block_rows = rows(d["x"], k)
                        at_least(sp, s_xt_ps, k - 1)
                        sp.dma_start(xb[:, u, :], block_rows).then_inc(s_x[u], 16)
                    if live[3]:
                        b, q = k - 3, (u + 1) % 2
                        ra, rb = rows(a_t, b), rows(b_t, b)
                        sp.wait_ge(s_ab, b + 1)
                        sp.dma_start(ra, ab[:, q, 0:H]).then_inc(s_st[q], 16)
                        sp.dma_start(rb, ab[:, q, H:2 * H]).then_inc(s_st[q], 16)
                staged(sp, step, 4)
                for q in range(2):
                    sp.wait_ge(s_st[q], NB // 2 * 32)

            @block.tensor
            def _(pe):
                def step(k, u, live):
                    if live[1]:
                        b, q = k - 1, (u + 1) % 2
                        pe.wait_ge(s_x[q], 16 * ((b - q) // 2 + 1) if isinstance(b, int) else 8 * (b - q) + 16)
                        at_least(pe, s_xt, b - 1)
                        pe.transpose(bank[q][:, 0:P], xb[:, q, :], ident).then_inc(s_xt_ps, 1)
                    if live[2]:
                        b, q = k - 2, u
                        pe.wait_ge(s_xt, b + 1)
                        at_least(pe, s_ab, b - 1)
                        pe.matmul(bank[2 + q][:, :], xt[:, q, :], wm1[:, :], start=True, stop=True).then_inc(s_ab_ps, 1)
                staged(pe, step, 3)

            @block.scalar
            def _(act):
                def step(k, u, live):
                    if live[0]:
                        act.wait_ge(s_xt_ps, k + 1)
                        at_least(act, s_ab_ps, k - 1)
                        act.copy(xt[:, u, :], bank[u][:, 0:P]).then_inc(s_xt, 1)
                staged(act, step, 1)

            @block.vector
            def _(dve):
                def step(k, u, live):
                    if live[0]:
                        dve.wait_ge(s_ab_ps, k + 1)
                        at_least(dve, s_st[u], 32 * ((k - u) // 2) if isinstance(k, int) else 16 * (k - u))
                        dve.tensor_tensor(ab[:, u, :], bank[2 + u][:, :], ab_bias[:, :], ALU.add).then_inc(s_ab, 1)
                staged(dve, step, 1)

        with ExitStack() as sx:
            def tmp(name, shape, dt=F32):
                return sx.enter_context(nc.sbuf_tensor(name, shape, dt))
            ia, ib = tmp("ia", [P, U, G], I32), tmp("ib", [P, U, G], I32)
            ga, gb = tmp("ga", [P, U, G, H]), tmp("gb", [P, U, G, H])
            keep = tmp("keep0", [P, U, T], BF16)
            h1, h2 = tmp("h1", [P, 2, 2, T]), tmp("h2", [P, 2, 2, T])
            sc = tmp("sc", [P, 2, 2, T])
            rowed = tmp("rowed", [P, 2, G, H])
            s_idx = sem("l0_idx")
            s_g = [sem(f"l0_gather{s}") for s in range(U)]
            s_keep = [sem(f"l0_keep{s}") for s in range(U)]
            s_st = [sem(f"l0_store{s}") for s in range(2)]
            s_pre, s_h1, s_w2, s_h2 = sem("l0_pre"), sem("l0_h1"), sem("l0_w2"), sem("l0_h2")
            s_scan, s_out_ps, s_out, s_zero = sem("l0_scan"), sem("l0_out_ps"), sem("l0_out"), sem("l0_zero")
            pre, hid, back = bank[0:2], bank[2:4], bank[4:6]
            block = sx.enter_context(nc.Block())

            @block.gpsimd
            def _(pool):
                def body(i):
                    for s in range(U):
                        t = i * U + s
                        pool.wait_ge(s_idx, t + 1)
                        at_least(pool, s_pre, 2 * t - 2 * U + 2)
                        pool.sem_inc(s_turn, 1)
                        for j in range(G):
                            pool.indirect_dma_start(ga[:, s, j, :], None, a_t, bass.IndirectOffsetOnAxis(
                                ap=ia[:, s, j:j + 1], axis=0)).then_inc(s_g[s], 16)
                            pool.indirect_dma_start(gb[:, s, j, :], None, b_t, bass.IndirectOffsetOnAxis(
                                ap=ib[:, s, j:j + 1], axis=0)).then_inc(s_g[s], 16)
                over(pool, body, IT)

            @block.sync
            def _(sp):
                def masks(t, s):
                    sp.dma_start(keep[:, s, :], keep_t[bass.ds(t * T, T)].partition_broadcast(P)).then_inc(s_keep[s], 16)
                for s in range(U):
                    masks(s, s)

                def body(i):
                    for s in range(U):
                        t = i * U + s
                        out = sum_t[bass.ds(t * T, T), :].rearrange("(j p) f -> p j f", p=P)
                        sp.wait_ge(s_out, 2 * t + 2)
                        sp.dma_start(out, rowed[:, s % 2, :, :]).then_inc(s_st[s % 2], 16)
                        if not (isinstance(i, int) and i > 0):
                            nxt = keep_t[bass.ds(t * T + U * T, T)].partition_broadcast(P)
                            sp.wait_ge(s_scan, 2 * t + 2)
                            sp.dma_start(keep[:, s, :], nxt).then_inc(s_keep[s], 16)
                over(sp, body, IT)
                for q in range(2):
                    sp.wait_ge(s_st[q], TILES // 2 * 16)

            @block.tensor
            def _(pe):
                def transpose_in(t, s, first=False):
                    pe.wait_ge(s_g[s], (t - s) * 32 + 128)
                    for h in range(2):
                        at_least(pe, s_h1, 2 * t - 2 + h + 1)
                        for r in (ga, gb):
                            for j in range(G):
                                last = pe.matmul(pre[h][:, P * j:P * j + P], r[:, s, j, P * h:P * h + P], ident,
                                                 is_transpose=True, start=(r is ga and j == 0),
                                                 stop=(r is gb and j == G - 1))
                        last.then_inc(s_pre, 1)

                def layer2(t, s):
                    q = s % 2
                    pe.wait_ge(s_h1, 2 * t + 2)
                    for m in range(2):
                        at_least(pe, s_h2, 2 * t - 2 + m + 1)
                        for k in range(2):
                            last = pe.matmul(hid[m][:, :], wm2[:, k, P * m:P * m + P], h1[:, q, k, :],
                                             start=(k == 0), stop=(k == 1))
                        last.then_inc(s_w2, 1)

                def transpose_out(t, s):
                    q = s % 2
                    pe.wait_ge(s_scan, 2 * t + 2)
                    for c in range(2):
                        at_least(pe, s_out, 2 * t - 2 + c + 1)
                        for jj in range(2):
                            for h in range(2):
                                j = 2 * c + jj
                                last = pe.transpose(back[c][:, H * jj + P * h:H * jj + P * h + P],
                                                    sc[:, q, h, P * j:P * j + P], ident)
                        last.then_inc(s_out_ps, 1)

                transpose_in(0, 0)

                def body(i):
                    for s in range(U):
                        t = i * U + s
                        if not (isinstance(i, int) and i > 0 and s == U - 1):
                            transpose_in(t + 1, (s + 1) % U)
                        layer2(t, s)
                        if not (isinstance(t, int) and t == 0):
                            transpose_out(t - 1, (s - 1) % U)
                over(pe, body, IT)
                transpose_out(TILES - 1, U - 1)

            @block.scalar
            def _(act):
                def relu1(t, s):
                    at_least(act, s_w2, 2 * t - 2)
                    for h in range(2):
                        act.wait_ge(s_pre, 2 * t + h + 1)
                        act.activation(h1[:, s % 2, h, :], pre[h][:, :], ACT.Relu).then_inc(s_h1, 1)

                def relu2(t, s):
                    for m in range(2):
                        act.wait_ge(s_w2, 2 * t + m + 1)
                        at_least(act, s_scan, 2 * t - 4 + m + 1)
                        act.activation(h2[:, s % 2, m, :], hid[m][:, :], ACT.Relu, bias=bm2[:, m:m + 1]).then_inc(s_h2, 1)

                def copy_out(t, s):
                    q = s % 2
                    at_least(act, s_st[q], ((t - q) // 2 * 16) if isinstance(t, int) else (t - q) * 8)
                    for c in range(2):
                        act.wait_ge(s_out_ps, 2 * t + c + 1)
                        act.copy(rowed[:, q, 2 * c:2 * c + 2, :].rearrange("p j f -> p (j f)"), back[c][:, :]).then_inc(s_out, 1)

                relu1(0, 0)

                def body(i):
                    for s in range(U):
                        t = i * U + s
                        if not (isinstance(i, int) and i > 0 and s == U - 1):
                            relu1(t + 1, (s + 1) % U)
                        relu2(t, s)
                        if not (isinstance(t, int) and t == 0):
                            copy_out(t - 1, (s - 1) % U)
                over(act, body, IT)
                copy_out(TILES - 1, U - 1)

            @block.vector
            def _(dve):
                dve.memset(sc[:, 1, :, T - 1:T], 0.0).then_inc(s_zero, 1)
                for s in range(U):
                    dve.tensor_copy(ia[:, s, :], src[:, G * s:G * s + G])
                    dve.tensor_copy(ib[:, s, :], dst[:, G * s:G * s + G]).then_inc(s_idx, 1)
                dve.wait_ge(s_zero, 1)

                def body(i):
                    for s in range(U):
                        t, q = i * U + s, s % 2
                        dve.wait_ge(s_keep[s], i * 16 + 16)
                        at_least(dve, s_out_ps, 2 * t - 2)
                        for h in range(2):
                            dve.wait_ge(s_h2, 2 * t + h + 1)
                            at_least(dve, s_scan, 2 * t - 2 + h + 1)
                            dve.tensor_tensor_scan(sc[:, q, h, :], keep[:, s, :], h2[:, q, h, :],
                                                   sc[:, 1 - q, h, T - 1:T], ALU.mult, ALU.add).then_inc(s_scan, 1)
                        if not (isinstance(i, int) and i > 0):
                            nxt = (i * U + U + s) * G
                            dve.tensor_scalar(ia[:, s, :], src[:, bass.ds(nxt, G)], 1.0, None, ALU.mult)
                            dve.tensor_scalar(ib[:, s, :], dst[:, bass.ds(nxt, G)], 1.0, None, ALU.mult).then_inc(s_idx, 1)
                over(dve, body, IT)

        with ExitStack() as sx:
            def tmp(name, shape, dt=F32):
                return sx.enter_context(nc.sbuf_tensor(name, shape, dt))
            hg = tmp("hg", [P, 2, H])
            ht = tmp("ht", [P, 2, H])
            bf = tmp("bf", [P, 2, D])
            agg = tmp("agg", [P, 2, D])
            xa, xr = tmp("xa", [P, 2, D]), tmp("xr", [P, 2, D])
            at = tmp("at", [P, 2, 2 * D])
            hn = tmp("hn", [P, 2, H])
            y1, y = tmp("y1", [P, 2, D]), tmp("y", [P, 2, D])
            st6, mv = tmp("st6", [P, 2, 6]), tmp("mv", [P, 2, 2])
            sd, rs = tmp("sd", [P, 2]), tmp("rs", [P, 2])
            z = tmp("z", [P, 2, D])
            zt, pr = tmp("zt", [P, 2, P]), tmp("pr", [P, 2, D])
            s_idx = sem("n1_idx")
            s_g = [sem(f"n1_gather{q}") for q in range(2)]
            s_xa = [sem(f"n1_xa{q}") for q in range(2)]
            s_xr = [sem(f"n1_xr{q}") for q in range(2)]
            s_zst = [sem(f"n1_zst{q}") for q in range(2)]
            s_pst = [sem(f"n1_pst{q}") for q in range(2)]
            (s_ht_ps, s_ht, s_m_ps, s_bf, s_agg, s_at_ps, s_at, s_h_ps, s_hn, s_u_ps, s_y1, s_y, s_st6, s_mv,
             s_sd, s_rs, s_z, s_zt_ps, s_zt, s_p_ps, s_p) = (sem("n1_" + x) for x in (
                 "ht_ps ht m_ps bf agg at_ps at h_ps hn u_ps y1 y st6 mv sd rs z zt_ps zt p_ps p").split())

            def loads(b, q, each=16):
                return each * ((b - q) // 2 + 1) if isinstance(b, int) else (each // 2) * (b - q) + each
            block = sx.enter_context(nc.Block())
            S = 8

            @block.gpsimd
            def _(pool):
                def step(k, u, live):
                    if live[0]:
                        pool.wait_ge(s_idx, k + 1)
                        at_least(pool, s_ht_ps, k - 1)
                        pool.sem_inc(s_turn, 1)
                        pool.indirect_dma_start(hg[:, u, :], None, sum_t, bass.IndirectOffsetOnAxis(
                            ap=idx[:, u:u + 1], axis=0)).then_inc(s_g[u], 16)
                staged(pool, step, 1)

            @block.sync
            def _(sp):
                def step(k, u, live):
                    v = 1 - u
                    if live[1]:
                        b = k - 1
                        r = rows(d["x"], b)
                        at_least(sp, s_at_ps, b - 1)
                        sp.dma_start(xa[:, v, :], r).then_inc(s_xa[v], 16)
                    if live[3]:
                        b = k - 3
                        r = rows(d["x"], b)
                        at_least(sp, s_y1, b - 1)
                        sp.dma_start(xr[:, v, :], r).then_inc(s_xr[v], 16)
                    if live[6]:
                        b = k - 6
                        r = rows(z_t, b)
                        sp.wait_ge(s_z, b + 1)
                        sp.dma_start(r, z[:, u, :]).then_inc(s_zst[u], 16)
                    if live[8]:
                        b = k - 8
                        r = rows(p_t, b)
                        sp.wait_ge(s_p, b + 1)
                        sp.dma_start(r, pr[:, u, :]).then_inc(s_pst[u], 16)
                staged(sp, step, 9)
                for q in range(2):
                    sp.wait_ge(s_zst[q], NB // 2 * 16)
                    sp.wait_ge(s_pst[q], NB // 2 * 16)

            @block.tensor
            def _(pe):
                def step(k, u, live):
                    v = 1 - u
                    if live[0]:
                        pe.wait_ge(s_g[u], loads(k, u))
                        at_least(pe, s_ht, k)
                        for h in range(2):
                            last = pe.transpose(bank[0][:, P * h:P * h + P], hg[:, u, P * h:P * h + P], ident)
                        last.then_inc(s_ht_ps, 1)
                    if live[1]:
                        b = k - 1
                        pe.wait_ge(s_ht, b + 1)
                        at_least(pe, s_agg, b)
                        for h in range(2):
                            last = pe.matmul(bank[1][:, 0:D], ht[:, v, P * h:P * h + P], wm3[:, h, :],
                                             start=(h == 0), stop=(h == 1))
                        last.then_inc(s_m_ps, 1)
                    if live[2]:
                        b = k - 2
                        pe.wait_ge(s_agg, b + 1)
                        pe.wait_ge(s_xa[u], loads(b, u))
                        at_least(pe, s_at, b)
                        pe.transpose(bank[2][:, 0:P], xa[:, u, :], ident)
                        pe.transpose(bank[2][:, P:2 * P], agg[:, u, :], ident).then_inc(s_at_ps, 1)
                    if live[3]:
                        b = k - 3
                        pe.wait_ge(s_at, b + 1)
                        at_least(pe, s_hn, 2 * b)
                        for m in range(2):
                            for h in range(2):
                                last = pe.matmul(bank[3][:, P * m:P * m + P], wn1[:, h, P * m:P * m + P],
                                                 at[:, v, P * h:P * h + P], start=(m == 0 and h == 0), stop=(m == 1 and h == 1))
                        last.then_inc(s_h_ps, 1)
                    if live[4]:
                        b = k - 4
                        pe.wait_ge(s_hn, 2 * b + 2)
                        at_least(pe, s_y, b)
                        for h in range(2):
                            last = pe.matmul(bank[4][:, 0:D], hn[:, u, P * h:P * h + P], wn2[:, h, :],
                                             start=(h == 0), stop=(h == 1))
                        last.then_inc(s_u_ps, 1)
                    if live[6]:
                        b = k - 6
                        pe.wait_ge(s_z, b + 1)
                        at_least(pe, s_zt, b)
                        pe.transpose(bank[5][:, 0:P], z[:, u, :], ident).then_inc(s_zt_ps, 1)
                    if live[7]:
                        b = k - 7
                        pe.wait_ge(s_zt, b + 1)
                        at_least(pe, s_p, b)
                        pe.matmul(bank[6][:, 0:D], zt[:, v, :], wd_s[:, 1, :], start=True, stop=True).then_inc(s_p_ps, 1)
                staged(pe, step, S)

            @block.scalar
            def _(act):
                def step(k, u, live):
                    v = 1 - u
                    if live[0]:
                        act.wait_ge(s_ht_ps, k + 1)
                        at_least(act, s_m_ps, k - 1)
                        act.copy(ht[:, u, :], bank[0][:, 0:H]).then_inc(s_ht, 1)
                    if live[2]:
                        b = k - 2
                        act.wait_ge(s_at_ps, b + 1)
                        at_least(act, s_h_ps, b - 1)
                        act.copy(at[:, u, :], bank[2][:, 0:2 * D]).then_inc(s_at, 1)
                    if live[3]:
                        b = k - 3
                        act.wait_ge(s_h_ps, b + 1)
                        at_least(act, s_u_ps, b - 1)
                        for m in range(2):
                            act.activation(hn[:, v, P * m:P * m + P], bank[3][:, P * m:P * m + P], ACT.Relu,
                                           bias=bn1[:, m:m + 1]).then_inc(s_hn, 1)
                    if live[5]:
                        b = k - 5
                        act.wait_ge(s_mv, b + 1)
                        at_least(act, s_rs, b - 1)
                        act.activation(sd[:, v:v + 1], mv[:, v, 1:2], ACT.Sqrt, bias=eps[:, :]).then_inc(s_sd, 1)
                    if live[6]:
                        b = k - 6
                        act.wait_ge(s_zt_ps, b + 1)
                        at_least(act, s_p_ps, b - 1)
                        act.copy(zt[:, u, :], bank[5][:, 0:P]).then_inc(s_zt, 1)
                    if live[7]:
                        b = k - 7
                        act.wait_ge(s_p_ps, b + 1)
                        at_least(act, s_pst[v], loads(b, v) - 16)
                        act.copy(pr[:, v, :], bank[6][:, 0:D]).then_inc(s_p, 1)
                staged(act, step, S)

            @block.vector
            def _(dve):
                def step(k, u, live):
                    v = 1 - u
                    if live[0]:
                        at_least(dve, s_g[u], loads(k, u) - 16)
                        dve.tensor_scalar(idx[:, u:u + 1], col(end_f, k), 1.0, None, ALU.mult).then_inc(s_idx, 1)
                    if live[2]:
                        b = k - 2
                        at_least(dve, s_agg, b - 1)
                        dve.tensor_scalar(bf[:, u, :], bm3[:, :], col(flag, b), None, ALU.mult).then_inc(s_bf, 1)
                        dve.wait_ge(s_m_ps, b + 1)
                        dve.wait_ge(s_bf, b + 1)
                        at_least(dve, s_at_ps, b - 1)
                        dve.scalar_tensor_tensor(agg[:, u, :], bank[1][:, 0:D], col(rcp, b), bf[:, u, :],
                                                 ALU.mult, ALU.add).then_inc(s_agg, 1)
                    if live[5]:
                        b = k - 5
                        dve.wait_ge(s_xr[v], loads(b, v))
                        at_least(dve, s_y, b - 1)
                        dve.scalar_tensor_tensor(y1[:, v, :], xr[:, v, :], 2.0, bn2[:, :], ALU.mult, ALU.add).then_inc(s_y1, 1)
                        dve.wait_ge(s_u_ps, b + 1)
                        dve.wait_ge(s_y1, b + 1)
                        at_least(dve, s_z, b - 1)
                        dve.tensor_tensor(y[:, v, :], bank[4][:, 0:D], y1[:, v, :], ALU.add).then_inc(s_y, 1)
                        dve.wait_ge(s_y, b + 1)
                        dve.bn_stats(st6[:, v, :], y[:, v, :]).then_inc(s_st6, 1)
                        dve.wait_ge(s_st6, b + 1)
                        at_least(dve, s_sd, b - 1)
                        dve.sem_inc(s_aggr, 1)
                        dve.bn_aggr(mv[:, v, :], st6[:, v, :]).then_inc(s_mv, 1)
                    if live[6]:
                        b = k - 6
                        dve.wait_ge(s_sd, b + 1)
                        dve.reciprocal(rs[:, u:u + 1], sd[:, u:u + 1]).then_inc(s_rs, 1)
                        dve.wait_ge(s_rs, b + 1)
                        at_least(dve, s_zst[u], loads(b, u) - 16)
                        at_least(dve, s_zt_ps, b - 1)
                        dve.tensor_scalar(z[:, u, :], y[:, u, :], mv[:, u, 0:1], rs[:, u:u + 1],
                                          ALU.subtract, ALU.mult).then_inc(s_z, 1)
                staged(dve, step, S)

        with ExitStack() as sx:
            def tmp(name, shape, dt=F32):
                return sx.enter_context(nc.sbuf_tensor(name, shape, dt))
            ia = tmp("ia1", [P, U, G], I32)
            gp = tmp("gp", [P, U, G, D])
            pen = tmp("pen1", [P, U, T], BF16)
            wt = tmp("wt", [1, U, T])
            sc = tmp("sc1", [P, 2, T])
            rowed = tmp("rowed1", [P, 2, G, D])
            s_idx = sem("l1_idx")
            s_g = [sem(f"l1_gather{s}") for s in range(U)]
            s_pen = [sem(f"l1_pen{s}") for s in range(U)]
            s_wt = [sem(f"l1_wt{s}") for s in range(U)]
            s_st = [sem(f"l1_store{s}") for s in range(2)]
            s_pre, s_scan, s_out_ps, s_out, s_zero = sem("l1_pre"), sem("l1_scan"), sem("l1_out_ps"), sem("l1_out"), sem("l1_zero")
            pre, back = bank[0:2], bank[2:4]
            block = sx.enter_context(nc.Block())

            @block.gpsimd
            def _(pool):
                def body(i):
                    for s in range(U):
                        t = i * U + s
                        pool.wait_ge(s_idx, t + 1)
                        at_least(pool, s_pre, t - U + 1)
                        pool.sem_inc(s_turn, 1)
                        for j in range(G):
                            pool.indirect_dma_start(gp[:, s, j, :], None, p_t, bass.IndirectOffsetOnAxis(
                                ap=ia[:, s, j:j + 1], axis=0)).then_inc(s_g[s], 16)
                over(pool, body, IT)

            @block.sync
            def _(sp):
                for s in range(U):
                    sp.dma_start(pen[:, s, :], pen_t[s * T:s * T + T].partition_broadcast(P)).then_inc(s_pen[s], 16)
                    sp.dma_start(wt[:, s, :], d["edge_weight"][:, s * T:s * T + T]).then_inc(s_wt[s], 16)

                def body(i):
                    for s in range(U):
                        t = i * U + s
                        out = max_t[bass.ds(t * T, T), :].rearrange("(j p) f -> p j f", p=P)
                        sp.wait_ge(s_out, t + 1)
                        sp.dma_start(out, rowed[:, s % 2, :, :]).then_inc(s_st[s % 2], 16)
                        if not (isinstance(i, int) and i > 0):
                            nxt = t * T + U * T
                            a, w = pen_t[bass.ds(nxt, T)].partition_broadcast(P), d["edge_weight"][:, bass.ds(nxt, T)]
                            sp.wait_ge(s_scan, t + 1)
                            sp.dma_start(pen[:, s, :], a).then_inc(s_pen[s], 16)
                            sp.dma_start(wt[:, s, :], w).then_inc(s_wt[s], 16)
                over(sp, body, IT)
                for q in range(2):
                    sp.wait_ge(s_st[q], TILES // 2 * 16)

            @block.tensor
            def _(pe):
                def message(t, s):
                    q = s % 2
                    at_least(pe, s_scan, t - 1)
                    pe.wait_ge(s_wt[s], (t - s) * 4 + 16)
                    pe.matmul(pre[q][:, :], ww[:, :], wt[:, s, :], start=True, stop=False)
                    pe.wait_ge(s_g[s], (t - s) * 16 + 64)
                    for j in range(G):
                        last = pe.matmul(pre[q][:, P * j:P * j + P], gp[:, s, j, :], ident, is_transpose=True,
                                         start=False, stop=(j == G - 1))
                    last.then_inc(s_pre, 1)

                def transpose_out(t, s):
                    q = s % 2
                    pe.wait_ge(s_scan, t + 1)
                    at_least(pe, s_out, t - 1)
                    for j in range(G):
                        last = pe.transpose(back[q][:, P * j:P * j + P], sc[:, q, P * j:P * j + P], ident)
                    last.then_inc(s_out_ps, 1)

                def body(i):
                    for s in range(U):
                        t = i * U + s
                        message(t, s)
                        if not (isinstance(t, int) and t == 0):
                            transpose_out(t - 1, (s - 1) % U)
                over(pe, body, IT)
                transpose_out(TILES - 1, U - 1)

            @block.scalar
            def _(act):
                def body(i):
                    for s in range(U):
                        t, q = i * U + s, s % 2
                        act.wait_ge(s_out_ps, t + 1)
                        at_least(act, s_st[q], ((t - q) // 2 * 16) if isinstance(t, int) else (t - q) * 8)
                        act.copy(rowed[:, q, :, :].rearrange("p j f -> p (j f)"), back[q][:, :]).then_inc(s_out, 1)
                over(act, body, IT)

            @block.vector
            def _(dve):
                dve.memset(sc[:, 1, T - 1:T], 0.0).then_inc(s_zero, 1)
                for s in range(U):
                    dve.tensor_copy(ia[:, s, :], src[:, G * s:G * s + G]).then_inc(s_idx, 1)
                dve.wait_ge(s_zero, 1)

                def body(i):
                    for s in range(U):
                        t, q = i * U + s, s % 2
                        dve.wait_ge(s_pen[s], i * 16 + 16)
                        at_least(dve, s_out_ps, t - 1)
                        dve.wait_ge(s_pre, t + 1)
                        at_least(dve, s_scan, t)
                        dve.tensor_tensor_scan(sc[:, q, :], pen[:, s, :], pre[q][:, :],
                                               sc[:, 1 - q, T - 1:T], ALU.add, ALU.max).then_inc(s_scan, 1)
                        if not (isinstance(i, int) and i > 0):
                            dve.tensor_scalar(ia[:, s, :], src[:, bass.ds((i * U + U + s) * G, G)], 1.0, None, ALU.mult).then_inc(s_idx, 1)
                over(dve, body, IT)

        with ExitStack() as sx:
            def tmp(name, shape, dt=F32):
                return sx.enter_context(nc.sbuf_tensor(name, shape, dt))
            mg, za, zr = tmp("mg", [P, 2, D]), tmp("za", [P, 2, D]), tmp("zr", [P, 2, D])
            zt = tmp("zt2", [P, 2, P])
            m1, m2, agg = tmp("m1", [P, 2, D]), tmp("m2", [P, 2, D]), tmp("agg2", [P, 2, D])
            zh = tmp("zh", [P, 2, P])
            at, hn = tmp("at2", [P, 2, P]), tmp("hn2", [P, 2, P])
            y1, y = tmp("y12", [P, 2, D]), tmp("y2", [P, 2, D])
            st6, mv = tmp("st62", [P, 2, 6]), tmp("mv2", [P, 2, 2])
            sd, rs = tmp("sd2", [P, 2]), tmp("rs2", [P, 2])
            o = tmp("o", [P, 2, D])
            s_idx = sem("n2_idx")
            s_g = [sem(f"n2_gather{q}") for q in range(2)]
            s_za = [sem(f"n2_za{q}") for q in range(2)]
            s_zr = [sem(f"n2_zr{q}") for q in range(2)]
            s_ost = [sem(f"n2_ost{q}") for q in range(2)]
            (s_zt_ps, s_zt, s_q_ps, s_m1, s_m2, s_agg, s_at_ps, s_at, s_h_ps, s_hn, s_u_ps, s_y1, s_y, s_st6, s_mv,
             s_sd, s_rs, s_o) = (sem("n2_" + x) for x in (
                 "zt_ps zt q_ps m1 m2 agg at_ps at h_ps hn u_ps y1 y st6 mv sd rs o").split())
            block = sx.enter_context(nc.Block())
            S = 7

            @block.gpsimd
            def _(pool):
                def step(k, u, live):
                    if live[0]:
                        pool.wait_ge(s_idx, k + 1)
                        at_least(pool, s_m1, k - 1)
                        pool.sem_inc(s_turn, 1)
                        pool.indirect_dma_start(mg[:, u, :], None, max_t, bass.IndirectOffsetOnAxis(
                            ap=idx[:, u:u + 1], axis=0)).then_inc(s_g[u], 16)
                staged(pool, step, 1)

            @block.sync
            def _(sp):
                def step(k, u, live):
                    v = 1 - u
                    if live[0]:
                        r = rows(z_t, k)
                        at_least(sp, s_zt_ps, k - 1)
                        sp.dma_start(za[:, u, :], r).then_inc(s_za[u], 16)
                    if live[3]:
                        b = k - 3
                        r = rows(z_t, b)
                        at_least(sp, s_y1, b - 1)
                        sp.dma_start(zr[:, v, :], r).then_inc(s_zr[v], 16)
                    if live[7]:
                        b = k - 7
                        r = rows(d["out"], b)
                        sp.wait_ge(s_o, b + 1)
                        sp.dma_start(r, o[:, v, :]).then_inc(s_ost[v], 16)
                staged(sp, step, 8)
                for q in range(2):
                    sp.wait_ge(s_ost[q], NB // 2 * 16)

            @block.tensor
            def _(pe):
                def step(k, u, live):
                    v = 1 - u
                    if live[0]:
                        pe.wait_ge(s_za[u], loads(k, u))
                        at_least(pe, s_zt, k)
                        pe.transpose(bank[0][:, 0:P], za[:, u, :], ident).then_inc(s_zt_ps, 1)
                    if live[1]:
                        b = k - 1
                        pe.wait_ge(s_zt, b + 1)
                        at_least(pe, s_m1, b)
                        pe.matmul(bank[1][:, 0:D], zt[:, v, :], wd_s[:, 0, :], start=True, stop=True).then_inc(s_q_ps, 1)
                    if live[2]:
                        b = k - 2
                        pe.wait_ge(s_agg, b + 1)
                        at_least(pe, s_at, 2 * b)
                        pe.transpose(bank[2][:, 0:P], agg[:, u, :], ident).then_inc(s_at_ps, 1)
                    if live[3]:
                        b = k - 3
                        pe.wait_ge(s_at, 2 * b + 2)
                        at_least(pe, s_hn, b)
                        pe.matmul(bank[3][:, 0:P], w1[:, 0, :], zh[:, v, :], start=True, stop=False)
                        pe.matmul(bank[3][:, 0:P], w1[:, 1, :], at[:, v, :], start=False, stop=True).then_inc(s_h_ps, 1)
                    if live[4]:
                        b = k - 4
                        pe.wait_ge(s_hn, b + 1)
                        at_least(pe, s_y, b)
                        pe.matmul(bank[4][:, 0:D], hn[:, u, :], w2[:, :], start=True, stop=True).then_inc(s_u_ps, 1)
                staged(pe, step, S)

            @block.scalar
            def _(act):
                def step(k, u, live):
                    v = 1 - u
                    if live[2]:
                        b = k - 2
                        act.wait_ge(s_zt, b + 1)
                        at_least(act, s_h_ps, b - 1)
                        act.copy(zh[:, u, :], zt[:, u, :]).then_inc(s_at, 1)
                        act.wait_ge(s_at_ps, b + 1)
                        act.copy(at[:, u, :], bank[2][:, 0:P]).then_inc(s_at, 1)
                    if live[0]:
                        act.wait_ge(s_zt_ps, k + 1)
                        at_least(act, s_q_ps, k - 1)
                        at_least(act, s_at, 2 * k - 2)
                        act.copy(zt[:, u, :], bank[0][:, 0:P]).then_inc(s_zt, 1)
                    if live[3]:
                        b = k - 3
                        act.wait_ge(s_h_ps, b + 1)
                        at_least(act, s_u_ps, b - 1)
                        act.activation(hn[:, v, :], bank[3][:, 0:P], ACT.Relu, bias=b1[:, :]).then_inc(s_hn, 1)
                    if live[5]:
                        b = k - 5
                        act.wait_ge(s_mv, b + 1)
                        at_least(act, s_rs, b - 1)
                        act.activation(sd[:, v:v + 1], mv[:, v, 1:2], ACT.Sqrt, bias=eps[:, :]).then_inc(s_sd, 1)
                staged(act, step, S)

            @block.vector
            def _(dve):
                def step(k, u, live):
                    v = 1 - u
                    if live[0]:
                        at_least(dve, s_g[u], loads(k, u) - 16)
                        dve.tensor_scalar(idx[:, u:u + 1], col(end_f, k), 1.0, None, ALU.mult).then_inc(s_idx, 1)
                    if live[2]:
                        b = k - 2
                        dve.wait_ge(s_g[u], loads(b, u))
                        dve.wait_ge(s_q_ps, b + 1)
                        at_least(dve, s_m2, b - 1)
                        dve.tensor_tensor(m1[:, u, :], bank[1][:, 0:D], mg[:, u, :], ALU.add).then_inc(s_m1, 1)
                        dve.wait_ge(s_m1, b + 1)
                        at_least(dve, s_agg, b - 1)
                        dve.tensor_tensor(m2[:, u, :], m1[:, u, :], bm[:, :], ALU.add).then_inc(s_m2, 1)
                        dve.wait_ge(s_m2, b + 1)
                        at_least(dve, s_at_ps, b - 1)
                        dve.tensor_scalar(agg[:, u, :], m2[:, u, :], col(flag, b), None, ALU.mult).then_inc(s_agg, 1)
                    if live[5]:
                        b = k - 5
                        dve.wait_ge(s_zr[v], loads(b, v))
                        at_least(dve, s_y, b - 1)
                        dve.tensor_tensor(y1[:, v, :], zr[:, v, :], b2[:, :], ALU.add).then_inc(s_y1, 1)
                        dve.wait_ge(s_u_ps, b + 1)
                        dve.wait_ge(s_y1, b + 1)
                        at_least(dve, s_o, b - 1)
                        dve.tensor_tensor(y[:, v, :], bank[4][:, 0:D], y1[:, v, :], ALU.add).then_inc(s_y, 1)
                        dve.wait_ge(s_y, b + 1)
                        dve.bn_stats(st6[:, v, :], y[:, v, :]).then_inc(s_st6, 1)
                        dve.wait_ge(s_st6, b + 1)
                        at_least(dve, s_sd, b - 1)
                        dve.sem_inc(s_aggr, 1)
                        dve.bn_aggr(mv[:, v, :], st6[:, v, :]).then_inc(s_mv, 1)
                    if live[6]:
                        b = k - 6
                        dve.wait_ge(s_sd, b + 1)
                        dve.reciprocal(rs[:, u:u + 1], sd[:, u:u + 1]).then_inc(s_rs, 1)
                        dve.wait_ge(s_rs, b + 1)
                        at_least(dve, s_ost[u], loads(b, u) - 16)
                        dve.tensor_scalar(o[:, u, :], y[:, u, :], mv[:, u, 0:1], rs[:, u:u + 1],
                                          ALU.subtract, ALU.mult).then_inc(s_o, 1)
                staged(dve, step, S)


WEIGHTS = ["L0_gnn_Wm1", "L0_gnn_bm1", "L0_gnn_Wm2", "L0_gnn_bm2", "L0_gnn_Wm3", "L0_gnn_bm3", "L0_gnn_Wn1",
           "L0_gnn_bn1", "L0_gnn_Wn2", "L0_gnn_bn2", "L1_gnn_Wm", "L1_gnn_bm", "L1_gnn_W1", "L1_gnn_b1",
           "L1_gnn_W2", "L1_gnn_b2"]


def kernel(**inputs):
    import numpy as _np
    import concourse.bacc as _bacc
    from concourse import mybir as _mybir
    from concourse.bass_utils import run_bass_kernel_spmd as _run

    def padded(a, size, fill):
        out = _np.full((size,) + a.shape[1:], fill, a.dtype)
        out[:a.shape[0]] = a
        return out

    def by_partition(a):
        return _np.ascontiguousarray(padded(a, EP, 0).reshape(ROWS, P).T)

    src, dst = _np.asarray(inputs["src"]), _np.asarray(inputs["dst"])
    dst_cur = padded(dst, EP, NP)
    dst_prev = _np.full((EP,), -1, dst.dtype)
    dst_prev[1:] = dst_cur[:-1]
    arrays = {
        "x": padded(_np.asarray(inputs["x"]), NP, 0),
        "src": by_partition(src),
        "dst": by_partition(dst),
        "dst_cur": dst_cur,
        "dst_prev": dst_prev,
        "dst_last": _np.ascontiguousarray(dst_cur[P - 1::P]),
        "dst_rows": dst_cur.reshape(ROWS, P),
        "edge_weight": padded(_np.asarray(inputs["edge_weight"]), EP, 0).reshape(1, EP),
    }
    for name in WEIGHTS:
        arrays[name] = _np.ascontiguousarray(inputs[name])
    for name in ("L0_gnn_bm2", "L0_gnn_bn1", "L1_gnn_b1"):
        arrays[name] = _np.ascontiguousarray(arrays[name].reshape(-1, P).T)
    nc = _bacc.Bacc("TRN2", target_bir_lowering=False, num_devices=1)
    d, feed = {}, {}
    for name, a in arrays.items():
        feed[f"in_{name}"] = a
        d[name] = nc.dram_tensor(f"in_{name}", a.shape, _mybir.dt.from_np(a.dtype), kind="ExternalInput").ap()
    d["out"] = nc.dram_tensor("out_rows", (NP, D), F32, kind="ExternalOutput").ap()
    program(nc, d)
    r = _run(nc, [feed], core_ids=[0])
    return r.results[0]["out_rows"][:N]
```

```python
from contextlib import ExitStack

import numpy as np

import concourse.bass as bass
from concourse import mybir
from concourse.alu_op_type import AluOpType as ALU

F32 = mybir.dt.float32
F32R = mybir.dt.float32r
BF16 = mybir.dt.bfloat16
I32 = mybir.dt.int32
ACT = mybir.ActivationFunctionType

N, E, D, H = 6250, 100000, 128, 256
P = 128
T = 512
G = T // P
U = 4
IT = -(-E // (T * U))
TILES = IT * U
EP = TILES * T
ROWS = EP // P
NB = -(-N // P)
NB += NB % 2
NP = NB * P
FAR = float(NP)
RESTART = -3.0e38
EPS = 1e-5
WIN = 64
SPAN_ROWS = EP // (2 * T)


def at_least(eng, sem, value):
    if isinstance(value, int) and value <= 0:
        return
    eng.wait_ge(sem, value)


def over(eng, body, count):
    body(0)
    with eng.Fori(1, count - 1) as i:
        body(i)
    body(count - 1)


def staged(eng, body, stages):
    lead = (stages + 3) // 2
    pairs = (NB + stages - 1 + 1) // 2
    full = NB // 2

    def pair(j, fixed):
        for u in range(2):
            k = 2 * j + u
            live = [not fixed or 0 <= k - s < NB for s in range(stages)]
            if any(live):
                body(k, u, live)

    for j in range(lead):
        pair(j, True)
    with eng.Fori(lead, full) as j:
        pair(j, False)
    for j in range(full, pairs):
        pair(j, True)


def col(t, i):
    return t[:, bass.ds(i, 1)] if not isinstance(i, int) else t[:, i:i + 1]


def rows(t, i, n=P):
    return t[n * i:n * i + n, :] if isinstance(i, int) else t[bass.ds(i * n, n), :]


def program(nc, d):
    ctx = ExitStack()
    with ctx:
        def sb(name, shape, dt=F32):
            return ctx.enter_context(nc.sbuf_tensor(name, shape, dt))

        def sem(name):
            return ctx.enter_context(nc.semaphore(name))

        def dram(name, shape, dt=F32):
            return nc.dram_tensor(name, shape, dt, kind="Internal").ap()

        a_t, b_t = dram("a_t", (NP, H)), dram("b_t", (NP, H))
        keep_t, pen_t = dram("keep_t", (EP,), BF16), dram("pen_t", (EP,), BF16)
        bh_t, bl_t = dram("bh_t", (NP, H)), dram("bl_t", (NP, H))
        rel_t = dram("rel_t", (EP,), BF16)
        sum_t = dram("sum_t", (EP, H))
        z_t, p_t = dram("z_t", (NP, D)), dram("p_t", (NP, D))
        max_t = dram("max_t", (EP, D))

        diag = sb("diag", [P, 2 * P])
        ident = diag[:, 1:P + 1]
        below = diag[:, 0:P]
        wrap = diag[:, P:2 * P]
        wm1 = sb("wm1", [P, 2 * H])
        wm2 = sb("wm2", [P, 2, H])
        wm2_hi, wm2_lo = sb("wm2_hi", [P, 2, H], F32R), sb("wm2_lo", [P, 2, H], F32R)
        wm3 = sb("wm3", [P, 2, D])
        wn1 = sb("wn1", [P, 2, H])
        wn2 = sb("wn2", [P, 2, D])
        wd_s = sb("wd_s", [P, 2, D])
        ww = sb("ww", [1, D])
        w1 = sb("w1", [P, 2, D])
        w2 = sb("w2", [P, D])
        ab_bias = sb("ab_bias", [P, 2 * H])
        bm2 = sb("bm2", [P, 2])
        bn1 = sb("bn1", [P, 2])
        b1 = sb("b1", [P, 1])
        bm3 = sb("bm3", [P, D])
        bn2 = sb("bn2", [P, D])
        bm = sb("bm", [P, D])
        b2 = sb("b2", [P, D])
        eps = sb("eps", [P, 1])
        node = sb("node", [P, NB])
        node_i = sb("node_i", [P, NB], I32)
        in_win, in_high = sb("in_win", [P, 1]), sb("in_high", [P, 1])
        tile_first = sb("tile_first", [1, TILES], I32)
        span = sb("span", [1, 1], I32)
        src = sb("src", [P, ROWS], I32)
        dst = sb("dst", [P, ROWS], I32)
        cnt = sb("cnt", [P, NB + 1])
        tiles_le = sb("tiles_le", [P, NB])
        fine = sb("fine", [P, NB])
        rcp = sb("rcp", [P, NB])
        flag = sb("flag", [P, NB])
        end_f = sb("end_f", [P, NB])
        idx = sb("idx", [P, 2], I32)

        s_turn, s_aggr = sem("pool_turn"), sem("dve_aggr")

        bank = [ctx.enter_context(nc.psum_tensor(f"bank{i}", [P, 512], F32)) for i in range(8)]

        with ExitStack() as sx:
            def tmp(name, shape, dt=F32):
                return sx.enter_context(nc.sbuf_tensor(name, shape, dt))
            W = EP // P
            cur_i, prev_i = tmp("cur_i", [P, W], I32), tmp("prev_i", [P, W], I32)
            cur, prev = tmp("cur", [P, W]), tmp("prev", [P, W])
            keep, pen = tmp("keep", [P, W], BF16), tmp("pen", [P, W], BF16)
            last_i, last = tmp("last_i", [P, ROWS], I32), tmp("last", [P, ROWS])
            hit = tmp("hit", [P, ROWS])
            row_i = tmp("row_i", [P, 2, P], I32)
            row_f, row_hit = tmp("row_f", [P, P]), tmp("row_hit", [P, P])
            s_diag, s_w, s_edges, s_iota = sem("s_diag"), sem("s_w"), sem("s_edges"), sem("s_iota")
            s_mask, s_mask_st = sem("s_mask"), sem("s_mask_st")
            s_cast, s_coarse, s_idx = sem("s_cast"), sem("s_coarse"), sem("s_idx")
            s_row = [sem("s_row0"), sem("s_row1")]
            s_rowf, s_hit, s_cnt, s_deg_ps, s_deg = sem("s_rowf"), sem("s_hit"), sem("s_cnt"), sem("s_deg_ps"), sem("s_deg")
            s_zero, s_span, s_two, s_rel = sem("s_zero"), sem("s_span"), sem("s_two"), sem("s_rel")
            two_i, two = tmp("two_i", [SPAN_ROWS, 2 * T], I32), tmp("two", [SPAN_ROWS, 2 * T])
            rel = tmp("rel", [SPAN_ROWS, 2 * T], BF16)
            tile_last = tmp("tile_last", [1, TILES], I32)
            first_f, spans = tmp("first_f", [1, TILES]), tmp("spans", [1, TILES])
            block = sx.enter_context(nc.Block())

            @block.sync
            def _(sp):
                sp.dma_start(cur_i[:, :], d["dst_cur"].rearrange("(p c) -> p c", p=P)).then_inc(s_edges, 16)
                sp.dma_start(prev_i[:, :], d["dst_prev"].rearrange("(p c) -> p c", p=P)).then_inc(s_edges, 16)
                sp.dma_start(last_i[:, :], d["dst_last"].partition_broadcast(P)).then_inc(s_edges, 16)
                sp.dma_start(src[:, :], d["src"]).then_inc(s_edges, 16)
                sp.dma_start(dst[:, :], d["dst"]).then_inc(s_edges, 16)
                sp.dma_start(two_i[:, :], d["dst_cur"].rearrange("(p c) -> p c", c=2 * T)).then_inc(s_two, 16)
                sp.dma_start(tile_first[:, :], d["tile_first"]).then_inc(s_two, 16)
                sp.dma_start(tile_last[:, :], d["tile_last"]).then_inc(s_two, 16)
                halves = {"L0_gnn_Wm1": wm1.rearrange("p (a n) -> p a n", a=2), "L0_gnn_Wm2": wm2, "L0_gnn_Wm3": wm3,
                          "L0_gnn_Wn1": wn1, "L0_gnn_Wn2": wn2, "L1_gnn_W1": w1}
                for name, t in halves.items():
                    sp.dma_start(t[:, :, :], d[name].rearrange("(a p) n -> p a n", p=P)).then_inc(s_w, 16)
                sp.dma_start(wd_s[:, :, :], d["L1_gnn_Wm"][0:2 * D, :].rearrange("(a p) n -> p a n", p=P)).then_inc(s_w, 16)
                sp.dma_start(ww[:, :], d["L1_gnn_Wm"][2 * D:2 * D + 1, :]).then_inc(s_w, 16)
                sp.dma_start(w2[:, :], d["L1_gnn_W2"]).then_inc(s_w, 16)
                sp.dma_start(ab_bias[:, H:2 * H], d["L0_gnn_bm1"].partition_broadcast(P)).then_inc(s_w, 16)
                for name, t in {"L0_gnn_bm3": bm3, "L0_gnn_bn2": bn2, "L1_gnn_bm": bm, "L1_gnn_b2": b2}.items():
                    sp.dma_start(t[:, :], d[name].partition_broadcast(P)).then_inc(s_w, 16)
                for name, t in {"L0_gnn_bm2": bm2, "L0_gnn_bn1": bn1, "L1_gnn_b1": b1}.items():
                    sp.dma_start(t[:, :], d[name]).then_inc(s_w, 16)
                sp.wait_ge(s_mask, 2)
                sp.dma_start(keep_t.rearrange("(p c) -> p c", p=P), keep[:, :]).then_inc(s_mask_st, 16)
                sp.dma_start(pen_t.rearrange("(p c) -> p c", p=P), pen[:, :]).then_inc(s_mask_st, 16)
                sp.wait_ge(s_rel, 2)
                sp.dma_start(rel_t.rearrange("(p c) -> p c", c=2 * T), rel[:, :]).then_inc(s_mask_st, 16)
                sp.wait_ge(s_mask_st, 48)
                sp.wait_ge(s_edges, 5 * 16)
                sp.wait_ge(s_w, 17 * 16)

            @block.gpsimd
            def _(pool):
                pool.memset(diag[:, :], 0.0).then_inc(s_diag, 1)
                pool.wait_ge(s_diag, 1)
                pool.affine_select(out=diag[:, :], in_=diag[:, :], compare_op=ALU.not_equal, fill=1.0, base=1,
                                   pattern=[[-1, 2 * P]], channel_multiplier=1).then_inc(s_diag, 1)
                pool.iota(node_i[:, :], pattern=[[P, NB]], base=0, channel_multiplier=1).then_inc(s_iota, 1)

                def fetch_row(b, q):
                    pool.wait_ge(s_idx, b + 1)
                    pool.sem_inc(s_turn, 1)
                    pool.indirect_dma_start(row_i[:, q, :], None, d["dst_rows"],
                                            bass.IndirectOffsetOnAxis(ap=idx[:, q:q + 1], axis=0)).then_inc(s_row[q], 16)
                staged(pool, lambda k, u, live: fetch_row(k, u), 1)

            @block.vector
            def _(dve):
                dve.memset(eps[:, :], EPS)
                dve.memset(ab_bias[:, 0:H], 0.0)
                dve.memset(cnt[:, 0:1], 0.0).then_inc(s_zero, 1)
                dve.wait_ge(s_edges, 5 * 16)
                dve.tensor_copy(cur[:, :], cur_i[:, :])
                dve.tensor_copy(prev[:, :], prev_i[:, :])
                dve.tensor_copy(last[:, :], last_i[:, :])
                dve.wait_ge(s_iota, 1)
                dve.tensor_copy(node[:, :], node_i[:, :]).then_inc(s_cast, 1)
                dve.wait_ge(s_cast, 1)
                dve.tensor_scalar(in_high[:, :], node[:, 0:1], float(WIN), float(WIN), ALU.is_ge, ALU.mult).then_inc(s_cast, 1)
                dve.wait_ge(s_cast, 2)
                dve.tensor_tensor(in_win[:, :], node[:, 0:1], in_high[:, :], ALU.subtract)
                dve.tensor_tensor(keep[:, :], cur[:, :], prev[:, :], ALU.is_equal).then_inc(s_mask, 1)
                dve.wait_ge(s_mask, 1)
                dve.tensor_scalar(pen[:, :], keep[:, :], -RESTART, RESTART, ALU.mult, ALU.add).then_inc(s_mask, 1)

                dve.wait_ge(s_two, 3 * 16)
                dve.tensor_copy(two[:, :], two_i[:, :]).then_inc(s_span, 1)
                dve.tensor_copy(first_f[:, :], tile_first[:, :]).then_inc(s_span, 1)
                dve.wait_ge(s_span, 2)
                for c in range(2):
                    dve.tensor_scalar(rel[:, T * c:T * c + T], two[:, T * c:T * c + T], two[:, T * c:T * c + 1],
                                      None, ALU.subtract).then_inc(s_rel, 1)
                dve.tensor_tensor(spans[:, :], tile_last[:, :], first_f[:, :], ALU.subtract).then_inc(s_span, 1)
                dve.wait_ge(s_span, 3)
                dve.reduce_max(first_f[:, 0:1], spans[:, :], mybir.AxisListType.X).then_inc(s_span, 1)
                dve.wait_ge(s_span, 4)
                dve.tensor_copy(span[:, :], first_f[:, 0:1])
                dve.wait_ge(s_w, 17 * 16)
                dve.tensor_copy(wm2_hi[:, :, :], wm2[:, :, :]).then_inc(s_span, 1)
                dve.wait_ge(s_span, 5)
                dve.tensor_tensor(wm2_lo[:, :, :], wm2[:, :, :], wm2_hi[:, :, :].bitcast(F32), ALU.subtract)

                def count(k, u, live):
                    if live[2]:
                        b = k - 2
                        dve.wait_ge(s_row[u], (k - u) * 8 if not isinstance(k, int) else 16 * (k // 2))
                        at_least(dve, s_hit, b)
                        dve.tensor_copy(row_f[:, :], row_i[:, u, :]).then_inc(s_rowf, 1)
                        dve.wait_ge(s_rowf, b + 1)
                        dve.tensor_scalar(row_hit[:, :], row_f[:, :], col(node, b), 0.0, ALU.is_le, ALU.add,
                                          accum_out=col(fine, b)).then_inc(s_hit, 1)
                    if live[0]:
                        at_least(dve, s_coarse, k)
                        dve.tensor_scalar(hit[:, :], last[:, :], col(node, k), 0.0, ALU.is_le, ALU.add,
                                          accum_out=col(tiles_le, k)).then_inc(s_coarse, 1)
                        dve.wait_ge(s_coarse, k + 1)
                        dve.tensor_scalar(idx[:, u:u + 1], col(tiles_le, k), 1.0, None, ALU.mult).then_inc(s_idx, 1)
                staged(dve, count, 3)
                dve.wait_ge(s_hit, NB)
                dve.wait_ge(s_coarse, NB)
                dve.scalar_tensor_tensor(cnt[:, 1:NB + 1], tiles_le[:, :], float(P), fine[:, :],
                                         ALU.mult, ALU.add).then_inc(s_cnt, 1)
                dve.wait_ge(s_cnt, 1)
                dve.tensor_scalar(end_f[:, :], cnt[:, 1:NB + 1], 1.0, 0.0, ALU.subtract, ALU.max).then_inc(s_cnt, 1)
                dve.wait_ge(s_deg_ps, 1)
                dve.tensor_tensor(fine[:, :], cnt[:, 1:NB + 1], bank[0][:, 0:NB], ALU.subtract).then_inc(s_deg, 1)
                dve.wait_ge(s_deg, 1)
                dve.tensor_scalar(flag[:, :], fine[:, :], 1.0, None, ALU.min).then_inc(s_deg, 1)
                dve.tensor_scalar(tiles_le[:, :], fine[:, :], 1.0, None, ALU.max).then_inc(s_deg, 1)
                dve.wait_ge(s_deg, 3)
                dve.reciprocal(rcp[:, :], tiles_le[:, :]).then_inc(s_deg, 1)

            @block.tensor
            def _(pe):
                pe.wait_ge(s_diag, 2)
                pe.wait_ge(s_cnt, 1)
                pe.wait_ge(s_zero, 1)
                pe.matmul(bank[0][:, 0:NB], below, cnt[:, 1:NB + 1], start=True, stop=False)
                pe.matmul(bank[0][:, 0:NB], wrap, cnt[:, 0:NB], start=False, stop=True).then_inc(s_deg_ps, 1)

        with ExitStack() as sx:
            def tmp(name, shape, dt=F32):
                return sx.enter_context(nc.sbuf_tensor(name, shape, dt))
            xb, xt, ab = tmp("xb", [P, 2, D]), tmp("xt", [P, 2, P]), tmp("ab", [P, 2, 2 * H])
            b_hi, b_lo = tmp("b_hi", [P, 2, H], F32R), tmp("b_lo", [P, 2, H], F32R)
            s_bh, s_bl = sem("s_bh"), sem("s_bl")
            s_x = [sem("s_x0"), sem("s_x1")]
            s_st = [sem("s_ab0"), sem("s_ab1")]
            s_xt_ps, s_xt, s_ab_ps, s_ab = sem("s_xt_ps"), sem("s_xt"), sem("s_ab_ps"), sem("s_ab")
            block = sx.enter_context(nc.Block())

            @block.sync
            def _(sp):
                def step(k, u, live):
                    if live[0]:
                        block_rows = rows(d["x"], k)
                        at_least(sp, s_xt_ps, k - 1)
                        sp.dma_start(xb[:, u, :], block_rows).then_inc(s_x[u], 16)
                    if live[3]:
                        b, q = k - 3, (u + 1) % 2
                        ra, rb, rh, rl = (rows(t, b) for t in (a_t, b_t, bh_t, bl_t))
                        sp.wait_ge(s_ab, b + 1)
                        sp.dma_start(ra, ab[:, q, 0:H]).then_inc(s_st[q], 16)
                        sp.dma_start(rb, ab[:, q, H:2 * H]).then_inc(s_st[q], 16)
                        sp.wait_ge(s_bl, b + 1)
                        sp.dma_start(rh, b_hi[:, q, :].bitcast(F32)).then_inc(s_st[q], 16)
                        sp.dma_start(rl, b_lo[:, q, :].bitcast(F32)).then_inc(s_st[q], 16)
                staged(sp, step, 4)
                for q in range(2):
                    sp.wait_ge(s_st[q], NB // 2 * 64)

            @block.tensor
            def _(pe):
                def step(k, u, live):
                    if live[1]:
                        b, q = k - 1, (u + 1) % 2
                        pe.wait_ge(s_x[q], 16 * ((b - q) // 2 + 1) if isinstance(b, int) else 8 * (b - q) + 16)
                        at_least(pe, s_xt, b - 1)
                        pe.transpose(bank[q][:, 0:P], xb[:, q, :], ident).then_inc(s_xt_ps, 1)
                    if live[2]:
                        b, q = k - 2, u
                        pe.wait_ge(s_xt, b + 1)
                        at_least(pe, s_ab, b - 1)
                        pe.matmul(bank[2 + q][:, :], xt[:, q, :], wm1[:, :], start=True, stop=True).then_inc(s_ab_ps, 1)
                staged(pe, step, 3)

            @block.scalar
            def _(act):
                def step(k, u, live):
                    if live[0]:
                        act.wait_ge(s_xt_ps, k + 1)
                        at_least(act, s_ab_ps, k - 1)
                        act.copy(xt[:, u, :], bank[u][:, 0:P]).then_inc(s_xt, 1)
                    if live[2]:
                        b = k - 2
                        act.wait_ge(s_ab, b + 1)
                        act.copy(b_hi[:, u, :], ab[:, u, H:2 * H]).then_inc(s_bh, 1)
                staged(act, step, 3)

            @block.vector
            def _(dve):
                def step(k, u, live):
                    if live[0]:
                        dve.wait_ge(s_ab_ps, k + 1)
                        at_least(dve, s_st[u], 64 * ((k - u) // 2) if isinstance(k, int) else 32 * (k - u))
                        dve.tensor_tensor(ab[:, u, :], bank[2 + u][:, :], ab_bias[:, :], ALU.add).then_inc(s_ab, 1)
                    if live[1]:
                        b, v = k - 1, 1 - u
                        dve.wait_ge(s_bh, b + 1)
                        dve.tensor_tensor(b_lo[:, v, :], ab[:, v, H:2 * H], b_hi[:, v, :].bitcast(F32),
                                          ALU.subtract).then_inc(s_bl, 1)
                staged(dve, step, 2)

        with ExitStack() as sx:
            def tmp(name, shape, dt=F32):
                return sx.enter_context(nc.sbuf_tensor(name, shape, dt))
            ia, ib = tmp("ia", [P, U, G], I32), tmp("ib", [P, U, G], I32)
            ga, gb = tmp("ga", [P, U, G, H]), tmp("gb", [P, U, G, H])
            keep, rel = tmp("keep0", [P, U, T], BF16), tmp("rel0", [P, U, T], BF16)
            win, sel = tmp("win", [P, U, H], F32R), tmp("sel", [P, 2, T], F32R)
            h1_hi, h1_lo = tmp("h1_hi", [P, 2, 2, T], F32R), tmp("h1_lo", [P, 2, 2, T], F32R)
            h1, h2 = tmp("h1", [P, 2, 2, T]), tmp("h2", [P, 2, 2, T])
            sc = tmp("sc", [P, 2, 2, T])
            rowed = tmp("rowed", [P, 2, G, H])
            hid, back = bank[2:4], bank[4:6]
            pre = [bank[0:2], bank[6:8]]
            s_idx = sem("l0_idx")
            s_g = [sem(f"l0_gather{s}") for s in range(U)]
            s_keep = [sem(f"l0_keep{s}") for s in range(U)]
            s_rel = [sem(f"l0_rel{s}") for s in range(U)]
            s_win = [sem(f"l0_win{s}") for s in range(U)]
            s_st = [sem(f"l0_store{s}") for s in range(2)]
            s_sel, s_pre, s_hi, s_lo, s_w2, s_h2 = (sem("l0_" + x) for x in "sel pre hi lo w2 h2".split())
            s_scan, s_out_ps, s_out, s_zero = sem("l0_scan"), sem("l0_out_ps"), sem("l0_out"), sem("l0_zero")
            s_h1 = s_lo

            def ends(i, s, ahead):
                return isinstance(i, int) and i * U + s + ahead >= TILES

            def either(eng, short, long):
                widest = eng.value_load(span[0:1, 0:1], min_val=0, max_val=N)
                with eng.If(widest < WIN):
                    short()
                with eng.Else():
                    long()
            block = sx.enter_context(nc.Block())

            @block.gpsimd
            def _(pool):
                def gathers(both):
                    def body(i):
                        for s in range(U):
                            t = i * U + s
                            pool.wait_ge(s_idx, t + 1)
                            at_least(pool, s_pre, 2 * t - 2 * U + 2)
                            pool.sem_inc(s_turn, 1)
                            for j in range(G):
                                pool.indirect_dma_start(ga[:, s, j, :], None, a_t, bass.IndirectOffsetOnAxis(
                                    ap=ia[:, s, j:j + 1], axis=0)).then_inc(s_g[s], 16)
                                if both:
                                    pool.indirect_dma_start(gb[:, s, j, :], None, b_t, bass.IndirectOffsetOnAxis(
                                        ap=ib[:, s, j:j + 1], axis=0)).then_inc(s_g[s], 16)
                    return lambda: over(pool, body, IT)
                either(pool, gathers(False), gathers(True))

            @block.sync
            def _(sp):
                def window(base, s):
                    for part, t in enumerate((bh_t, bl_t)):
                        sp.dma_start(win[WIN * part:WIN * part + WIN, s, :].bitcast(F32),
                                     t[bass.ds(base, WIN), :]).then_inc(s_win[s], 16)

                def loads(short):
                    def run():
                        for s in range(U):
                            sp.dma_start(keep[:, s, :], keep_t[T * s:T * s + T].partition_broadcast(P)).then_inc(s_keep[s], 16)
                            if short:
                                sp.dma_start(rel[:, s, :], rel_t[T * s:T * s + T].partition_broadcast(P)).then_inc(s_rel[s], 16)
                                window(sp.value_load(tile_first[0:1, s:s + 1], min_val=0, max_val=N - 1), s)

                        def body(i):
                            for s in range(U):
                                t = i * U + s
                                if not ends(i, s, U):
                                    nxt = t + U
                                    kr = keep_t[bass.ds(nxt * T, T)].partition_broadcast(P)
                                    if short:
                                        rr = rel_t[bass.ds(nxt * T, T)].partition_broadcast(P)
                                        base = sp.value_load(tile_first[0:1, bass.ds(nxt, 1)], min_val=0, max_val=N - 1)
                                        sp.wait_ge(s_pre, 2 * t + 2)
                                        sp.dma_start(rel[:, s, :], rr).then_inc(s_rel[s], 16)
                                        window(base, s)
                                    sp.wait_ge(s_scan, 2 * t + 2)
                                    sp.dma_start(keep[:, s, :], kr).then_inc(s_keep[s], 16)
                                out = sum_t[bass.ds(t * T, T), :].rearrange("(j p) f -> p j f", p=P)
                                sp.wait_ge(s_out, 2 * t + 2)
                                sp.dma_start(out, rowed[:, s % 2, :, :]).then_inc(s_st[s % 2], 16)
                        over(sp, body, IT)
                    return run
                either(sp, loads(True), loads(False))
                for q in range(2):
                    sp.wait_ge(s_st[q], TILES // 2 * 16)

            @block.tensor
            def _(pe):
                def turned(banks, r, s, h, start, stop):
                    for j in range(G):
                        last = pe.matmul(banks[h][:, P * j:P * j + P], r[:, s, j, P * h:P * h + P], ident,
                                         is_transpose=True, start=(start and j == 0), stop=(stop and j == G - 1))
                    return last

                def pre_long(t, s):
                    q = s % 2
                    pe.wait_ge(s_g[s], (t - s) * 32 + 128)
                    for h in range(2):
                        at_least(pe, s_h1, 2 * t - 4 + h + 1)
                        turned(pre[q], ga, s, h, True, False)
                        turned(pre[q], gb, s, h, False, True).then_inc(s_pre, 1)

                def pre_short(t, s):
                    q = s % 2
                    pe.wait_ge(s_sel, t + 1)
                    pe.wait_ge(s_win[s], (t - s) * 8 + 32)
                    pe.wait_ge(s_g[s], (t - s) * 16 + 64)
                    for h in range(2):
                        at_least(pe, s_lo, 2 * t - 4 + h + 1)
                        pe.matmul(pre[q][h][:, :], win[:, s, P * h:P * h + P], sel[:, q, :], start=True, stop=False)
                        turned(pre[q], ga, s, h, False, True).then_inc(s_pre, 1)

                def layer2_long(t, s):
                    q = s % 2
                    pe.wait_ge(s_h1, 2 * t + 2)
                    for m in range(2):
                        at_least(pe, s_h2, 2 * t - 2 + m + 1)
                        for k in range(2):
                            last = pe.matmul(hid[m][:, :], wm2[:, k, P * m:P * m + P], h1[:, q, k, :],
                                             start=(k == 0), stop=(k == 1))
                        last.then_inc(s_w2, 1)

                def layer2_short(t, s):
                    q = s % 2
                    pe.wait_ge(s_lo, 2 * t + 2)
                    for m in range(2):
                        at_least(pe, s_h2, 2 * t - 2 + m + 1)
                        pairs = [(w, r, k) for w, r in ((wm2_hi, h1_hi), (wm2_lo, h1_hi), (wm2_hi, h1_lo)) for k in range(2)]
                        for n, (w, r, k) in enumerate(pairs):
                            last = pe.matmul(hid[m][:, :], w[:, k, P * m:P * m + P], r[:, q, k, :],
                                             start=(n == 0), stop=(n == len(pairs) - 1))
                        last.then_inc(s_w2, 1)

                def transpose_out(t, s):
                    q = s % 2
                    pe.wait_ge(s_scan, 2 * t + 2)
                    for c in range(2):
                        at_least(pe, s_out, 2 * t - 2 + c + 1)
                        for jj in range(2):
                            for h in range(2):
                                j = 2 * c + jj
                                last = pe.transpose(back[c][:, H * jj + P * h:H * jj + P * h + P],
                                                    sc[:, q, h, P * j:P * j + P], ident)
                        last.then_inc(s_out_ps, 1)

                def tiles(pre_of, layer2):
                    def run():
                        pre_of(0, 0)

                        def body(i):
                            for s in range(U):
                                t = i * U + s
                                if not ends(i, s, 1):
                                    pre_of(t + 1, (s + 1) % U)
                                layer2(t, s)
                                if not (isinstance(t, int) and t == 0):
                                    transpose_out(t - 1, (s - 1) % U)
                        over(pe, body, IT)
                        transpose_out(TILES - 1, U - 1)
                    return run
                either(pe, tiles(pre_short, layer2_short), tiles(pre_long, layer2_long))

            @block.scalar
            def _(act):
                def relu1_long(t, s):
                    q = s % 2
                    at_least(act, s_w2, 2 * t - 2)
                    for h in range(2):
                        act.wait_ge(s_pre, 2 * t + h + 1)
                        act.activation(h1[:, q, h, :], pre[q][h][:, :], ACT.Relu).then_inc(s_h1, 1)

                def relu1_short(t, s):
                    q = s % 2
                    at_least(act, s_w2, 2 * t - 2)
                    for h in range(2):
                        act.wait_ge(s_pre, 2 * t + h + 1)
                        act.activation(h1_hi[:, q, h, :], pre[q][h][:, :], ACT.Relu).then_inc(s_hi, 1)

                def relu2(t, s):
                    for m in range(2):
                        act.wait_ge(s_w2, 2 * t + m + 1)
                        at_least(act, s_scan, 2 * t - 4 + m + 1)
                        act.activation(h2[:, s % 2, m, :], hid[m][:, :], ACT.Relu, bias=bm2[:, m:m + 1]).then_inc(s_h2, 1)

                def copy_out(t, s):
                    q = s % 2
                    at_least(act, s_st[q], ((t - q) // 2 * 16) if isinstance(t, int) else (t - q) * 8)
                    for c in range(2):
                        act.wait_ge(s_out_ps, 2 * t + c + 1)
                        act.copy(rowed[:, q, 2 * c:2 * c + 2, :].rearrange("p j f -> p (j f)"), back[c][:, :]).then_inc(s_out, 1)

                def tiles(relu1):
                    def run():
                        relu1(0, 0)

                        def body(i):
                            for s in range(U):
                                t = i * U + s
                                if not ends(i, s, 1):
                                    relu1(t + 1, (s + 1) % U)
                                relu2(t, s)
                                if not (isinstance(t, int) and t == 0):
                                    copy_out(t - 1, (s - 1) % U)
                        over(act, body, IT)
                        copy_out(TILES - 1, U - 1)
                    return run
                either(act, tiles(relu1_short), tiles(relu1_long))

            @block.vector
            def _(dve):
                dve.memset(sc[:, 1, :, T - 1:T], 0.0).then_inc(s_zero, 1)
                for s in range(U):
                    dve.tensor_copy(ia[:, s, :], src[:, G * s:G * s + G])
                    dve.tensor_copy(ib[:, s, :], dst[:, G * s:G * s + G]).then_inc(s_idx, 1)
                dve.wait_ge(s_zero, 1)

                def selection(i, t, s):
                    dve.wait_ge(s_rel[s], i * 16 + 16)
                    at_least(dve, s_pre, 2 * t - 2)
                    dve.tensor_scalar(sel[:, s % 2, :], rel[:, s, :], in_win[:, :], None, ALU.is_equal).then_inc(s_sel, 1)

                def low_part(t, s):
                    q = s % 2
                    for h in range(2):
                        dve.wait_ge(s_hi, 2 * t + h + 1)
                        dve.scalar_tensor_tensor(h1_lo[:, q, h, :], pre[q][h][:, :], 0.0, h1_hi[:, q, h, :].bitcast(F32),
                                                 ALU.max, ALU.subtract).then_inc(s_lo, 1)

                def scans(t, i, s):
                    q = s % 2
                    dve.wait_ge(s_keep[s], i * 16 + 16)
                    at_least(dve, s_out_ps, 2 * t - 2)
                    for h in range(2):
                        dve.wait_ge(s_h2, 2 * t + h + 1)
                        at_least(dve, s_scan, 2 * t - 2 + h + 1)
                        dve.tensor_tensor_scan(sc[:, q, h, :], keep[:, s, :], h2[:, q, h, :],
                                               sc[:, 1 - q, h, T - 1:T], ALU.mult, ALU.add).then_inc(s_scan, 1)

                def tiles(short):
                    def run():
                        if short:
                            selection(0, 0, 0)
                            selection(0, 1, 1)
                            low_part(0, 0)

                        def body(i):
                            for s in range(U):
                                t = i * U + s
                                if short and not ends(i, s, 1):
                                    low_part(t + 1, (s + 1) % U)
                                if short and not ends(i, s, 2):
                                    selection(i + (s + 2) // U, t + 2, (s + 2) % U)
                                scans(t, i, s)
                                if not ends(i, s, U):
                                    nxt = (i * U + U + s) * G
                                    dve.tensor_scalar(ia[:, s, :], src[:, bass.ds(nxt, G)], 1.0, None, ALU.mult)
                                    dve.tensor_scalar(ib[:, s, :], dst[:, bass.ds(nxt, G)], 1.0, None, ALU.mult).then_inc(s_idx, 1)
                        over(dve, body, IT)
                    return run
                either(dve, tiles(True), tiles(False))

        with ExitStack() as sx:
            def tmp(name, shape, dt=F32):
                return sx.enter_context(nc.sbuf_tensor(name, shape, dt))
            hg = tmp("hg", [P, 2, H])
            ht = tmp("ht", [P, 2, H])
            bf = tmp("bf", [P, 2, D])
            agg = tmp("agg", [P, 2, D])
            xa, xr = tmp("xa", [P, 2, D]), tmp("xr", [P, 2, D])
            at = tmp("at", [P, 2, 2 * D])
            hn = tmp("hn", [P, 2, H])
            y1, y = tmp("y1", [P, 2, D]), tmp("y", [P, 2, D])
            st6, mv = tmp("st6", [P, 2, 6]), tmp("mv", [P, 2, 2])
            sd, rs = tmp("sd", [P, 2]), tmp("rs", [P, 2])
            z = tmp("z", [P, 2, D])
            zt, pr = tmp("zt", [P, 2, P]), tmp("pr", [P, 2, D])
            s_idx = sem("n1_idx")
            s_g = [sem(f"n1_gather{q}") for q in range(2)]
            s_xa = [sem(f"n1_xa{q}") for q in range(2)]
            s_xr = [sem(f"n1_xr{q}") for q in range(2)]
            s_zst = [sem(f"n1_zst{q}") for q in range(2)]
            s_pst = [sem(f"n1_pst{q}") for q in range(2)]
            (s_ht_ps, s_ht, s_m_ps, s_bf, s_agg, s_at_ps, s_at, s_h_ps, s_hn, s_u_ps, s_y1, s_y, s_st6, s_mv,
             s_sd, s_rs, s_z, s_zt_ps, s_zt, s_p_ps, s_p) = (sem("n1_" + x) for x in (
                 "ht_ps ht m_ps bf agg at_ps at h_ps hn u_ps y1 y st6 mv sd rs z zt_ps zt p_ps p").split())

            def loads(b, q, each=16):
                return each * ((b - q) // 2 + 1) if isinstance(b, int) else (each // 2) * (b - q) + each
            block = sx.enter_context(nc.Block())
            S = 8

            @block.gpsimd
            def _(pool):
                def step(k, u, live):
                    if live[0]:
                        pool.wait_ge(s_idx, k + 1)
                        at_least(pool, s_ht_ps, k - 1)
                        pool.sem_inc(s_turn, 1)
                        pool.indirect_dma_start(hg[:, u, :], None, sum_t, bass.IndirectOffsetOnAxis(
                            ap=idx[:, u:u + 1], axis=0)).then_inc(s_g[u], 16)
                staged(pool, step, 1)

            @block.sync
            def _(sp):
                def step(k, u, live):
                    v = 1 - u
                    if live[1]:
                        b = k - 1
                        r = rows(d["x"], b)
                        at_least(sp, s_at_ps, b - 1)
                        sp.dma_start(xa[:, v, :], r).then_inc(s_xa[v], 16)
                    if live[3]:
                        b = k - 3
                        r = rows(d["x"], b)
                        at_least(sp, s_y1, b - 1)
                        sp.dma_start(xr[:, v, :], r).then_inc(s_xr[v], 16)
                    if live[6]:
                        b = k - 6
                        r = rows(z_t, b)
                        sp.wait_ge(s_z, b + 1)
                        sp.dma_start(r, z[:, u, :]).then_inc(s_zst[u], 16)
                    if live[8]:
                        b = k - 8
                        r = rows(p_t, b)
                        sp.wait_ge(s_p, b + 1)
                        sp.dma_start(r, pr[:, u, :]).then_inc(s_pst[u], 16)
                staged(sp, step, 9)
                for q in range(2):
                    sp.wait_ge(s_zst[q], NB // 2 * 16)
                    sp.wait_ge(s_pst[q], NB // 2 * 16)

            @block.tensor
            def _(pe):
                def step(k, u, live):
                    v = 1 - u
                    if live[0]:
                        pe.wait_ge(s_g[u], loads(k, u))
                        at_least(pe, s_ht, k)
                        for h in range(2):
                            last = pe.transpose(bank[0][:, P * h:P * h + P], hg[:, u, P * h:P * h + P], ident)
                        last.then_inc(s_ht_ps, 1)
                    if live[1]:
                        b = k - 1
                        pe.wait_ge(s_ht, b + 1)
                        at_least(pe, s_agg, b)
                        for h in range(2):
                            last = pe.matmul(bank[1][:, 0:D], ht[:, v, P * h:P * h + P], wm3[:, h, :],
                                             start=(h == 0), stop=(h == 1))
                        last.then_inc(s_m_ps, 1)
                    if live[2]:
                        b = k - 2
                        pe.wait_ge(s_agg, b + 1)
                        pe.wait_ge(s_xa[u], loads(b, u))
                        at_least(pe, s_at, b)
                        pe.transpose(bank[2][:, 0:P], xa[:, u, :], ident)
                        pe.transpose(bank[2][:, P:2 * P], agg[:, u, :], ident).then_inc(s_at_ps, 1)
                    if live[3]:
                        b = k - 3
                        pe.wait_ge(s_at, b + 1)
                        at_least(pe, s_hn, 2 * b)
                        for m in range(2):
                            for h in range(2):
                                last = pe.matmul(bank[3][:, P * m:P * m + P], wn1[:, h, P * m:P * m + P],
                                                 at[:, v, P * h:P * h + P], start=(m == 0 and h == 0), stop=(m == 1 and h == 1))
                        last.then_inc(s_h_ps, 1)
                    if live[4]:
                        b = k - 4
                        pe.wait_ge(s_hn, 2 * b + 2)
                        at_least(pe, s_y, b)
                        for h in range(2):
                            last = pe.matmul(bank[4][:, 0:D], hn[:, u, P * h:P * h + P], wn2[:, h, :],
                                             start=(h == 0), stop=(h == 1))
                        last.then_inc(s_u_ps, 1)
                    if live[6]:
                        b = k - 6
                        pe.wait_ge(s_z, b + 1)
                        at_least(pe, s_zt, b)
                        pe.transpose(bank[5][:, 0:P], z[:, u, :], ident).then_inc(s_zt_ps, 1)
                    if live[7]:
                        b = k - 7
                        pe.wait_ge(s_zt, b + 1)
                        at_least(pe, s_p, b)
                        pe.matmul(bank[6][:, 0:D], zt[:, v, :], wd_s[:, 1, :], start=True, stop=True).then_inc(s_p_ps, 1)
                staged(pe, step, S)

            @block.scalar
            def _(act):
                def step(k, u, live):
                    v = 1 - u
                    if live[0]:
                        act.wait_ge(s_ht_ps, k + 1)
                        at_least(act, s_m_ps, k - 1)
                        act.copy(ht[:, u, :], bank[0][:, 0:H]).then_inc(s_ht, 1)
                    if live[2]:
                        b = k - 2
                        act.wait_ge(s_at_ps, b + 1)
                        at_least(act, s_h_ps, b - 1)
                        act.copy(at[:, u, :], bank[2][:, 0:2 * D]).then_inc(s_at, 1)
                    if live[3]:
                        b = k - 3
                        act.wait_ge(s_h_ps, b + 1)
                        at_least(act, s_u_ps, b - 1)
                        for m in range(2):
                            act.activation(hn[:, v, P * m:P * m + P], bank[3][:, P * m:P * m + P], ACT.Relu,
                                           bias=bn1[:, m:m + 1]).then_inc(s_hn, 1)
                    if live[5]:
                        b = k - 5
                        act.wait_ge(s_mv, b + 1)
                        at_least(act, s_rs, b - 1)
                        act.activation(sd[:, v:v + 1], mv[:, v, 1:2], ACT.Sqrt, bias=eps[:, :]).then_inc(s_sd, 1)
                    if live[6]:
                        b = k - 6
                        act.wait_ge(s_zt_ps, b + 1)
                        at_least(act, s_p_ps, b - 1)
                        act.copy(zt[:, u, :], bank[5][:, 0:P]).then_inc(s_zt, 1)
                    if live[7]:
                        b = k - 7
                        act.wait_ge(s_p_ps, b + 1)
                        at_least(act, s_pst[v], loads(b, v) - 16)
                        act.copy(pr[:, v, :], bank[6][:, 0:D]).then_inc(s_p, 1)
                staged(act, step, S)

            @block.vector
            def _(dve):
                def step(k, u, live):
                    v = 1 - u
                    if live[0]:
                        at_least(dve, s_g[u], loads(k, u) - 16)
                        dve.tensor_scalar(idx[:, u:u + 1], col(end_f, k), 1.0, None, ALU.mult).then_inc(s_idx, 1)
                    if live[2]:
                        b = k - 2
                        at_least(dve, s_agg, b - 1)
                        dve.tensor_scalar(bf[:, u, :], bm3[:, :], col(flag, b), None, ALU.mult).then_inc(s_bf, 1)
                        dve.wait_ge(s_m_ps, b + 1)
                        dve.wait_ge(s_bf, b + 1)
                        at_least(dve, s_at_ps, b - 1)
                        dve.scalar_tensor_tensor(agg[:, u, :], bank[1][:, 0:D], col(rcp, b), bf[:, u, :],
                                                 ALU.mult, ALU.add).then_inc(s_agg, 1)
                    if live[5]:
                        b = k - 5
                        dve.wait_ge(s_xr[v], loads(b, v))
                        at_least(dve, s_y, b - 1)
                        dve.scalar_tensor_tensor(y1[:, v, :], xr[:, v, :], 2.0, bn2[:, :], ALU.mult, ALU.add).then_inc(s_y1, 1)
                        dve.wait_ge(s_u_ps, b + 1)
                        dve.wait_ge(s_y1, b + 1)
                        at_least(dve, s_z, b - 1)
                        dve.tensor_tensor(y[:, v, :], bank[4][:, 0:D], y1[:, v, :], ALU.add).then_inc(s_y, 1)
                        dve.wait_ge(s_y, b + 1)
                        dve.bn_stats(st6[:, v, :], y[:, v, :]).then_inc(s_st6, 1)
                        dve.wait_ge(s_st6, b + 1)
                        at_least(dve, s_sd, b - 1)
                        dve.sem_inc(s_aggr, 1)
                        dve.bn_aggr(mv[:, v, :], st6[:, v, :]).then_inc(s_mv, 1)
                    if live[6]:
                        b = k - 6
                        dve.wait_ge(s_sd, b + 1)
                        dve.reciprocal(rs[:, u:u + 1], sd[:, u:u + 1]).then_inc(s_rs, 1)
                        dve.wait_ge(s_rs, b + 1)
                        at_least(dve, s_zst[u], loads(b, u) - 16)
                        at_least(dve, s_zt_ps, b - 1)
                        dve.tensor_scalar(z[:, u, :], y[:, u, :], mv[:, u, 0:1], rs[:, u:u + 1],
                                          ALU.subtract, ALU.mult).then_inc(s_z, 1)
                staged(dve, step, S)

        with ExitStack() as sx:
            def tmp(name, shape, dt=F32):
                return sx.enter_context(nc.sbuf_tensor(name, shape, dt))
            ia = tmp("ia1", [P, U, G], I32)
            gp = tmp("gp", [P, U, G, D])
            pen = tmp("pen1", [P, U, T], BF16)
            wt = tmp("wt", [1, U, T])
            sc = tmp("sc1", [P, 2, T])
            rowed = tmp("rowed1", [P, 2, G, D])
            s_idx = sem("l1_idx")
            s_g = [sem(f"l1_gather{s}") for s in range(U)]
            s_pen = [sem(f"l1_pen{s}") for s in range(U)]
            s_wt = [sem(f"l1_wt{s}") for s in range(U)]
            s_st = [sem(f"l1_store{s}") for s in range(2)]
            s_pre, s_scan, s_out_ps, s_out, s_zero = sem("l1_pre"), sem("l1_scan"), sem("l1_out_ps"), sem("l1_out"), sem("l1_zero")
            pre, back = bank[0:2], bank[2:4]
            block = sx.enter_context(nc.Block())

            @block.gpsimd
            def _(pool):
                def body(i):
                    for s in range(U):
                        t = i * U + s
                        pool.wait_ge(s_idx, t + 1)
                        at_least(pool, s_pre, t - U + 1)
                        pool.sem_inc(s_turn, 1)
                        for j in range(G):
                            pool.indirect_dma_start(gp[:, s, j, :], None, p_t, bass.IndirectOffsetOnAxis(
                                ap=ia[:, s, j:j + 1], axis=0)).then_inc(s_g[s], 16)
                over(pool, body, IT)

            @block.sync
            def _(sp):
                for s in range(U):
                    sp.dma_start(pen[:, s, :], pen_t[s * T:s * T + T].partition_broadcast(P)).then_inc(s_pen[s], 16)
                    sp.dma_start(wt[:, s, :], d["edge_weight"][:, s * T:s * T + T]).then_inc(s_wt[s], 16)

                def body(i):
                    for s in range(U):
                        t = i * U + s
                        out = max_t[bass.ds(t * T, T), :].rearrange("(j p) f -> p j f", p=P)
                        sp.wait_ge(s_out, t + 1)
                        sp.dma_start(out, rowed[:, s % 2, :, :]).then_inc(s_st[s % 2], 16)
                        if not (isinstance(i, int) and i > 0):
                            nxt = t * T + U * T
                            a, w = pen_t[bass.ds(nxt, T)].partition_broadcast(P), d["edge_weight"][:, bass.ds(nxt, T)]
                            sp.wait_ge(s_scan, t + 1)
                            sp.dma_start(pen[:, s, :], a).then_inc(s_pen[s], 16)
                            sp.dma_start(wt[:, s, :], w).then_inc(s_wt[s], 16)
                over(sp, body, IT)
                for q in range(2):
                    sp.wait_ge(s_st[q], TILES // 2 * 16)

            @block.tensor
            def _(pe):
                def message(t, s):
                    q = s % 2
                    at_least(pe, s_scan, t - 1)
                    pe.wait_ge(s_wt[s], (t - s) * 4 + 16)
                    pe.matmul(pre[q][:, :], ww[:, :], wt[:, s, :], start=True, stop=False)
                    pe.wait_ge(s_g[s], (t - s) * 16 + 64)
                    for j in range(G):
                        last = pe.matmul(pre[q][:, P * j:P * j + P], gp[:, s, j, :], ident, is_transpose=True,
                                         start=False, stop=(j == G - 1))
                    last.then_inc(s_pre, 1)

                def transpose_out(t, s):
                    q = s % 2
                    pe.wait_ge(s_scan, t + 1)
                    at_least(pe, s_out, t - 1)
                    for j in range(G):
                        last = pe.transpose(back[q][:, P * j:P * j + P], sc[:, q, P * j:P * j + P], ident)
                    last.then_inc(s_out_ps, 1)

                def body(i):
                    for s in range(U):
                        t = i * U + s
                        message(t, s)
                        if not (isinstance(t, int) and t == 0):
                            transpose_out(t - 1, (s - 1) % U)
                over(pe, body, IT)
                transpose_out(TILES - 1, U - 1)

            @block.scalar
            def _(act):
                def body(i):
                    for s in range(U):
                        t, q = i * U + s, s % 2
                        act.wait_ge(s_out_ps, t + 1)
                        at_least(act, s_st[q], ((t - q) // 2 * 16) if isinstance(t, int) else (t - q) * 8)
                        act.copy(rowed[:, q, :, :].rearrange("p j f -> p (j f)"), back[q][:, :]).then_inc(s_out, 1)
                over(act, body, IT)

            @block.vector
            def _(dve):
                dve.memset(sc[:, 1, T - 1:T], 0.0).then_inc(s_zero, 1)
                for s in range(U):
                    dve.tensor_copy(ia[:, s, :], src[:, G * s:G * s + G]).then_inc(s_idx, 1)
                dve.wait_ge(s_zero, 1)

                def body(i):
                    for s in range(U):
                        t, q = i * U + s, s % 2
                        dve.wait_ge(s_pen[s], i * 16 + 16)
                        at_least(dve, s_out_ps, t - 1)
                        dve.wait_ge(s_pre, t + 1)
                        at_least(dve, s_scan, t)
                        dve.tensor_tensor_scan(sc[:, q, :], pen[:, s, :], pre[q][:, :],
                                               sc[:, 1 - q, T - 1:T], ALU.add, ALU.max).then_inc(s_scan, 1)
                        if not (isinstance(i, int) and i > 0):
                            dve.tensor_scalar(ia[:, s, :], src[:, bass.ds((i * U + U + s) * G, G)], 1.0, None, ALU.mult).then_inc(s_idx, 1)
                over(dve, body, IT)

        with ExitStack() as sx:
            def tmp(name, shape, dt=F32):
                return sx.enter_context(nc.sbuf_tensor(name, shape, dt))
            mg, za, zr = tmp("mg", [P, 2, D]), tmp("za", [P, 2, D]), tmp("zr", [P, 2, D])
            zt = tmp("zt2", [P, 2, P])
            m1, m2, agg = tmp("m1", [P, 2, D]), tmp("m2", [P, 2, D]), tmp("agg2", [P, 2, D])
            zh = tmp("zh", [P, 2, P])
            at, hn = tmp("at2", [P, 2, P]), tmp("hn2", [P, 2, P])
            y1, y = tmp("y12", [P, 2, D]), tmp("y2", [P, 2, D])
            st6, mv = tmp("st62", [P, 2, 6]), tmp("mv2", [P, 2, 2])
            sd, rs = tmp("sd2", [P, 2]), tmp("rs2", [P, 2])
            o = tmp("o", [P, 2, D])
            s_idx = sem("n2_idx")
            s_g = [sem(f"n2_gather{q}") for q in range(2)]
            s_za = [sem(f"n2_za{q}") for q in range(2)]
            s_zr = [sem(f"n2_zr{q}") for q in range(2)]
            s_ost = [sem(f"n2_ost{q}") for q in range(2)]
            (s_zt_ps, s_zt, s_q_ps, s_m1, s_m2, s_agg, s_at_ps, s_at, s_h_ps, s_hn, s_u_ps, s_y1, s_y, s_st6, s_mv,
             s_sd, s_rs, s_o) = (sem("n2_" + x) for x in (
                 "zt_ps zt q_ps m1 m2 agg at_ps at h_ps hn u_ps y1 y st6 mv sd rs o").split())
            block = sx.enter_context(nc.Block())
            S = 7

            @block.gpsimd
            def _(pool):
                def step(k, u, live):
                    if live[0]:
                        pool.wait_ge(s_idx, k + 1)
                        at_least(pool, s_m1, k - 1)
                        pool.sem_inc(s_turn, 1)
                        pool.indirect_dma_start(mg[:, u, :], None, max_t, bass.IndirectOffsetOnAxis(
                            ap=idx[:, u:u + 1], axis=0)).then_inc(s_g[u], 16)
                staged(pool, step, 1)

            @block.sync
            def _(sp):
                def step(k, u, live):
                    v = 1 - u
                    if live[0]:
                        r = rows(z_t, k)
                        at_least(sp, s_zt_ps, k - 1)
                        sp.dma_start(za[:, u, :], r).then_inc(s_za[u], 16)
                    if live[3]:
                        b = k - 3
                        r = rows(z_t, b)
                        at_least(sp, s_y1, b - 1)
                        sp.dma_start(zr[:, v, :], r).then_inc(s_zr[v], 16)
                    if live[7]:
                        b = k - 7
                        r = rows(d["out"], b)
                        sp.wait_ge(s_o, b + 1)
                        sp.dma_start(r, o[:, v, :]).then_inc(s_ost[v], 16)
                staged(sp, step, 8)
                for q in range(2):
                    sp.wait_ge(s_ost[q], NB // 2 * 16)

            @block.tensor
            def _(pe):
                def step(k, u, live):
                    v = 1 - u
                    if live[0]:
                        pe.wait_ge(s_za[u], loads(k, u))
                        at_least(pe, s_zt, k)
                        pe.transpose(bank[0][:, 0:P], za[:, u, :], ident).then_inc(s_zt_ps, 1)
                    if live[1]:
                        b = k - 1
                        pe.wait_ge(s_zt, b + 1)
                        at_least(pe, s_m1, b)
                        pe.matmul(bank[1][:, 0:D], zt[:, v, :], wd_s[:, 0, :], start=True, stop=True).then_inc(s_q_ps, 1)
                    if live[2]:
                        b = k - 2
                        pe.wait_ge(s_agg, b + 1)
                        at_least(pe, s_at, 2 * b)
                        pe.transpose(bank[2][:, 0:P], agg[:, u, :], ident).then_inc(s_at_ps, 1)
                    if live[3]:
                        b = k - 3
                        pe.wait_ge(s_at, 2 * b + 2)
                        at_least(pe, s_hn, b)
                        pe.matmul(bank[3][:, 0:P], w1[:, 0, :], zh[:, v, :], start=True, stop=False)
                        pe.matmul(bank[3][:, 0:P], w1[:, 1, :], at[:, v, :], start=False, stop=True).then_inc(s_h_ps, 1)
                    if live[4]:
                        b = k - 4
                        pe.wait_ge(s_hn, b + 1)
                        at_least(pe, s_y, b)
                        pe.matmul(bank[4][:, 0:D], hn[:, u, :], w2[:, :], start=True, stop=True).then_inc(s_u_ps, 1)
                staged(pe, step, S)

            @block.scalar
            def _(act):
                def step(k, u, live):
                    v = 1 - u
                    if live[2]:
                        b = k - 2
                        act.wait_ge(s_zt, b + 1)
                        at_least(act, s_h_ps, b - 1)
                        act.copy(zh[:, u, :], zt[:, u, :]).then_inc(s_at, 1)
                        act.wait_ge(s_at_ps, b + 1)
                        act.copy(at[:, u, :], bank[2][:, 0:P]).then_inc(s_at, 1)
                    if live[0]:
                        act.wait_ge(s_zt_ps, k + 1)
                        at_least(act, s_q_ps, k - 1)
                        at_least(act, s_at, 2 * k - 2)
                        act.copy(zt[:, u, :], bank[0][:, 0:P]).then_inc(s_zt, 1)
                    if live[3]:
                        b = k - 3
                        act.wait_ge(s_h_ps, b + 1)
                        at_least(act, s_u_ps, b - 1)
                        act.activation(hn[:, v, :], bank[3][:, 0:P], ACT.Relu, bias=b1[:, :]).then_inc(s_hn, 1)
                    if live[5]:
                        b = k - 5
                        act.wait_ge(s_mv, b + 1)
                        at_least(act, s_rs, b - 1)
                        act.activation(sd[:, v:v + 1], mv[:, v, 1:2], ACT.Sqrt, bias=eps[:, :]).then_inc(s_sd, 1)
                staged(act, step, S)

            @block.vector
            def _(dve):
                def step(k, u, live):
                    v = 1 - u
                    if live[0]:
                        at_least(dve, s_g[u], loads(k, u) - 16)
                        dve.tensor_scalar(idx[:, u:u + 1], col(end_f, k), 1.0, None, ALU.mult).then_inc(s_idx, 1)
                    if live[2]:
                        b = k - 2
                        dve.wait_ge(s_g[u], loads(b, u))
                        dve.wait_ge(s_q_ps, b + 1)
                        at_least(dve, s_m2, b - 1)
                        dve.tensor_tensor(m1[:, u, :], bank[1][:, 0:D], mg[:, u, :], ALU.add).then_inc(s_m1, 1)
                        dve.wait_ge(s_m1, b + 1)
                        at_least(dve, s_agg, b - 1)
                        dve.tensor_tensor(m2[:, u, :], m1[:, u, :], bm[:, :], ALU.add).then_inc(s_m2, 1)
                        dve.wait_ge(s_m2, b + 1)
                        at_least(dve, s_at_ps, b - 1)
                        dve.tensor_scalar(agg[:, u, :], m2[:, u, :], col(flag, b), None, ALU.mult).then_inc(s_agg, 1)
                    if live[5]:
                        b = k - 5
                        dve.wait_ge(s_zr[v], loads(b, v))
                        at_least(dve, s_y, b - 1)
                        dve.tensor_tensor(y1[:, v, :], zr[:, v, :], b2[:, :], ALU.add).then_inc(s_y1, 1)
                        dve.wait_ge(s_u_ps, b + 1)
                        dve.wait_ge(s_y1, b + 1)
                        at_least(dve, s_o, b - 1)
                        dve.tensor_tensor(y[:, v, :], bank[4][:, 0:D], y1[:, v, :], ALU.add).then_inc(s_y, 1)
                        dve.wait_ge(s_y, b + 1)
                        dve.bn_stats(st6[:, v, :], y[:, v, :]).then_inc(s_st6, 1)
                        dve.wait_ge(s_st6, b + 1)
                        at_least(dve, s_sd, b - 1)
                        dve.sem_inc(s_aggr, 1)
                        dve.bn_aggr(mv[:, v, :], st6[:, v, :]).then_inc(s_mv, 1)
                    if live[6]:
                        b = k - 6
                        dve.wait_ge(s_sd, b + 1)
                        dve.reciprocal(rs[:, u:u + 1], sd[:, u:u + 1]).then_inc(s_rs, 1)
                        dve.wait_ge(s_rs, b + 1)
                        at_least(dve, s_ost[u], loads(b, u) - 16)
                        dve.tensor_scalar(o[:, u, :], y[:, u, :], mv[:, u, 0:1], rs[:, u:u + 1],
                                          ALU.subtract, ALU.mult).then_inc(s_o, 1)
                staged(dve, step, S)


WEIGHTS = ["L0_gnn_Wm1", "L0_gnn_bm1", "L0_gnn_Wm2", "L0_gnn_bm2", "L0_gnn_Wm3", "L0_gnn_bm3", "L0_gnn_Wn1",
           "L0_gnn_bn1", "L0_gnn_Wn2", "L0_gnn_bn2", "L1_gnn_Wm", "L1_gnn_bm", "L1_gnn_W1", "L1_gnn_b1",
           "L1_gnn_W2", "L1_gnn_b2"]


def kernel(**inputs):
    import numpy as _np
    import concourse.bacc as _bacc
    from concourse import mybir as _mybir
    from concourse.bass_utils import run_bass_kernel_spmd as _run

    def padded(a, size, fill):
        out = _np.full((size,) + a.shape[1:], fill, a.dtype)
        out[:a.shape[0]] = a
        return out

    def by_partition(a):
        return _np.ascontiguousarray(padded(a, EP, 0).reshape(ROWS, P).T)

    src, dst = _np.asarray(inputs["src"]), _np.asarray(inputs["dst"])
    dst_cur = padded(dst, EP, NP)
    dst_prev = _np.full((EP,), -1, dst.dtype)
    dst_prev[1:] = dst_cur[:-1]
    arrays = {
        "x": padded(_np.asarray(inputs["x"]), NP, 0),
        "src": by_partition(src),
        "dst": by_partition(dst),
        "dst_cur": dst_cur,
        "dst_prev": dst_prev,
        "dst_last": _np.ascontiguousarray(dst_cur[P - 1::P]),
        "dst_rows": dst_cur.reshape(ROWS, P),
        "tile_first": _np.ascontiguousarray(dst_cur[::T]).reshape(1, TILES),
        "tile_last": _np.append(dst[T - 1::T], dst[-1:]).reshape(1, TILES),
        "edge_weight": padded(_np.asarray(inputs["edge_weight"]), EP, 0).reshape(1, EP),
    }
    for name in WEIGHTS:
        arrays[name] = _np.ascontiguousarray(inputs[name])
    for name in ("L0_gnn_bm2", "L0_gnn_bn1", "L1_gnn_b1"):
        arrays[name] = _np.ascontiguousarray(arrays[name].reshape(-1, P).T)
    nc = _bacc.Bacc("TRN2", target_bir_lowering=False, num_devices=1)
    d, feed = {}, {}
    for name, a in arrays.items():
        feed[f"in_{name}"] = a
        d[name] = nc.dram_tensor(f"in_{name}", a.shape, _mybir.dt.from_np(a.dtype), kind="ExternalInput").ap()
    d["out"] = nc.dram_tensor("out_rows", (NP, D), F32, kind="ExternalOutput").ap()
    program(nc, d)
    r = _run(nc, [feed], core_ids=[0])
    return r.results[0]["out_rows"][:N]
```

```python
from contextlib import ExitStack

import numpy as np

import concourse.bass as bass
from concourse import mybir
from concourse.alu_op_type import AluOpType as ALU

F32 = mybir.dt.float32
F32R = mybir.dt.float32r
BF16 = mybir.dt.bfloat16
I32 = mybir.dt.int32
ACT = mybir.ActivationFunctionType

N, E, D, H = 6250, 100000, 128, 256
P = 128
T = 512
G = T // P
U = 4
IT = -(-E // (T * U))
TILES = IT * U
EP = TILES * T
ROWS = EP // P
NB = -(-N // P)
NB += NB % 2
NP = NB * P
FAR = float(NP)
RESTART = -3.0e38
EPS = 1e-5
AHEAD = 2
LATE = sum(1 for _ in range(U + AHEAD, EP // T, U))
WIN = 64
SPAN_ROWS = EP // (2 * T)


def at_least(eng, sem, value):
    if isinstance(value, int) and value <= 0:
        return
    eng.wait_ge(sem, value)


def over(eng, body, count):
    body(0)
    with eng.Fori(1, count - 1) as i:
        body(i)
    body(count - 1)


def staged(eng, body, stages):
    lead = (stages + 3) // 2
    pairs = (NB + stages - 1 + 1) // 2
    full = NB // 2

    def pair(j, fixed):
        for u in range(2):
            k = 2 * j + u
            live = [not fixed or 0 <= k - s < NB for s in range(stages)]
            if any(live):
                body(k, u, live)

    for j in range(lead):
        pair(j, True)
    with eng.Fori(lead, full) as j:
        pair(j, False)
    for j in range(full, pairs):
        pair(j, True)


def col(t, i):
    return t[:, bass.ds(i, 1)] if not isinstance(i, int) else t[:, i:i + 1]


def rows(t, i, n=P):
    return t[n * i:n * i + n, :] if isinstance(i, int) else t[bass.ds(i * n, n), :]


def program(nc, d):
    ctx = ExitStack()
    with ctx:
        def sb(name, shape, dt=F32):
            return ctx.enter_context(nc.sbuf_tensor(name, shape, dt))

        def sem(name):
            return ctx.enter_context(nc.semaphore(name))

        def dram(name, shape, dt=F32):
            return nc.dram_tensor(name, shape, dt, kind="Internal").ap()

        a_t = dram("a_t", (NP, H))
        bb_t = dram("bb_t", (NP, 2 * H))
        keep_t, pen_t = dram("keep_t", (EP,), BF16), dram("pen_t", (EP,), BF16)
        rel_t = dram("rel_t", (EP,), BF16)
        scan_t = dram("scan_t", (EP * H // D, D))
        sum_t, max_t = scan_t.rearrange("(e h) f -> e (h f)", h=H // D), scan_t[0:EP, :]
        z_t, p_t = dram("z_t", (NP, D)), dram("p_t", (NP, D))

        diag = sb("diag", [P, 2 * P])
        ident = diag[:, 1:P + 1]
        below = diag[:, 0:P]
        wrap = diag[:, P:2 * P]
        wm1 = sb("wm1", [P, 2 * H])
        wm2 = sb("wm2", [P, 2, H])
        wm2_hi, wm2_lo = sb("wm2_hi", [P, 2, H], F32R), sb("wm2_lo", [P, 2, H], F32R)
        wm3 = sb("wm3", [P, 2, D])
        wn1 = sb("wn1", [P, 2, H])
        wn2 = sb("wn2", [P, 2, D])
        wd_s = sb("wd_s", [P, 2, D])
        ww = sb("ww", [1, D])
        w1 = sb("w1", [P, 2, D])
        w2 = sb("w2", [P, D])
        bm1 = sb("bm1", [P, H])
        bm2 = sb("bm2", [P, 2])
        bn1 = sb("bn1", [P, 2])
        b1 = sb("b1", [P, 1])
        bm3 = sb("bm3", [P, D])
        bn2 = sb("bn2", [P, D])
        bm = sb("bm", [P, D])
        b2 = sb("b2", [P, D])
        eps = sb("eps", [P, 1])
        node = sb("node", [P, NB])
        node_i = sb("node_i", [P, NB], I32)
        in_win, in_high = sb("in_win", [P, 1]), sb("in_high", [P, 1])
        tile_first = sb("tile_first", [1, TILES], I32)
        span = sb("span", [1, 1], I32)
        late = sb("late", [1, 1], I32)
        src = sb("src", [P, ROWS], I32)
        dst = sb("dst", [P, ROWS], I32)
        cnt = sb("cnt", [P, NB + 1])
        last_i, last = sb("last_i", [P, ROWS], I32), sb("last", [P, ROWS])
        tiles_le = sb("tiles_le", [P, NB])
        fine = sb("fine", [P, NB])
        flag = sb("flag", [P, NB])
        rcp = sb("rcp", [P, NB])
        end_f = sb("end_f", [P, NB + 2])
        idx = sb("idx", [P, 2], I32)

        s_turn, s_aggr, s_act_turn = sem("pool_turn"), sem("dve_aggr"), sem("act_turn")

        bank = [ctx.enter_context(nc.psum_tensor(f"bank{i}", [P, 512], F32)) for i in range(8)]

        with ExitStack() as sx:
            def tmp(name, shape, dt=F32):
                return sx.enter_context(nc.sbuf_tensor(name, shape, dt))
            W = EP // P
            cur_i, prev_i = tmp("cur_i", [P, W], I32), tmp("prev_i", [P, W], I32)
            cur, prev = tmp("cur", [P, W]), tmp("prev", [P, W])
            keep, pen = tmp("keep", [P, W], BF16), tmp("pen", [P, W], BF16)
            two_i, two = tmp("two_i", [SPAN_ROWS, 2 * T], I32), tmp("two", [SPAN_ROWS, 2 * T])
            rel = tmp("rel", [SPAN_ROWS, 2 * T], BF16)
            tile_last = tmp("tile_last", [1, TILES], I32)
            first_f, tile_last_f = tmp("first_f", [1, TILES]), tmp("tile_last_f", [1, TILES])
            spans, widest = tmp("spans", [1, TILES]), tmp("widest", [1, 1])
            trails, latest, late_f = tmp("trails", [1, LATE]), tmp("latest", [1, 1]), tmp("late_f", [1, 1])
            C, IN = 5, NB // 10
            xb, xt = tmp("xb", [P, 2 * C, D]), tmp("xt", [P, 2, P])
            a_s, b_s = tmp("a_s", [P, 2 * C, H]), tmp("b_s", [P, 2, H])
            bb_s = tmp("bb_s", [P, 2 * C, 2, H], F32R)
            s_diag, s_edges, s_iota, s_wm1, s_bm1, s_w = (sem("p_" + x) for x in "diag edges iota wm1 bm1 w".split())
            s_cast, s_mask, s_rel, s_mask_st, s_span, s_wm2 = (sem("p_" + x) for x in "cast mask rel mask_st span wm2".split())
            s_x = [sem(f"n0_x{h}") for h in range(2)]
            s_ast = [sem(f"n0_ast{h}") for h in range(2)]
            s_bst = [sem(f"n0_bst{h}") for h in range(2)]
            s_xt_ps, s_xt, s_ab_ps, s_a, s_b, s_bh, s_bl = (sem("n0_" + x) for x in "xt_ps xt ab_ps a b bh bl".split())
            block = sx.enter_context(nc.Block())

            def past(i, s, ahead):
                return isinstance(i, int) and i * 2 * C + s + ahead >= NB

            @block.gpsimd
            def _(pool):
                pool.memset(diag[:, :], 0.0).then_inc(s_diag, 1)
                pool.wait_ge(s_diag, 1)
                pool.affine_select(out=diag[:, :], in_=diag[:, :], compare_op=ALU.not_equal, fill=1.0, base=1,
                                   pattern=[[-1, 2 * P]], channel_multiplier=1).then_inc(s_diag, 1)
                pool.iota(node_i[:, :], pattern=[[P, NB]], base=0, channel_multiplier=1).then_inc(s_iota, 1)
                loads = [
                    (cur_i[:, :], d["dst_cur"].rearrange("(p c) -> p c", p=P)),
                    (prev_i[:, :], d["dst_prev"].rearrange("(p c) -> p c", p=P)),
                    (two_i[:, :], d["dst_cur"].rearrange("(p c) -> p c", c=2 * T)),
                    (tile_first[:, :], d["tile_first"]),
                    (tile_last[:, :], d["tile_last"]),
                    (last_i[:, :], d["dst_last"].partition_broadcast(P)),
                ]
                for out, in_ in loads:
                    pool.dma_start(out, in_).then_inc(s_edges, 16)
                weights = [(t[:, :, :], d[name].rearrange("(a p) n -> p a n", p=P)) for name, t in (
                    ("L0_gnn_Wm2", wm2), ("L0_gnn_Wm3", wm3), ("L0_gnn_Wn1", wn1), ("L0_gnn_Wn2", wn2),
                    ("L1_gnn_W1", w1))]
                weights += [(wd_s[:, :, :], d["L1_gnn_Wm"][0:2 * D, :].rearrange("(a p) n -> p a n", p=P)),
                            (ww[:, :], d["L1_gnn_Wm"][2 * D:2 * D + 1, :]), (w2[:, :], d["L1_gnn_W2"]),
                            (src[:, :], d["src"]), (dst[:, :], d["dst"])]
                weights += [(t[:, :], d[name].partition_broadcast(P)) for name, t in (
                    ("L0_gnn_bm3", bm3), ("L0_gnn_bn2", bn2), ("L1_gnn_bm", bm), ("L1_gnn_b2", b2))]
                weights += [(t[:, :], d[name]) for name, t in (
                    ("L0_gnn_bm2", bm2), ("L0_gnn_bn1", bn1), ("L1_gnn_b1", b1))]
                for out, in_ in weights:
                    pool.dma_start(out, in_).then_inc(s_w, 16)
                pool.wait_ge(s_mask, 2)
                pool.dma_start(keep_t.rearrange("(p c) -> p c", p=P), keep[:, :]).then_inc(s_mask_st, 16)
                pool.dma_start(pen_t.rearrange("(p c) -> p c", p=P), pen[:, :]).then_inc(s_mask_st, 16)
                pool.wait_ge(s_rel, 2)
                pool.dma_start(rel_t.rearrange("(p c) -> p c", c=2 * T), rel[:, :]).then_inc(s_mask_st, 16)
                pool.wait_ge(s_mask_st, 48)
                pool.wait_ge(s_w, 16 * len(weights))

            @block.sync
            def _(sp):
                sp.dma_start(wm1[:, :].rearrange("p (a n) -> p a n", a=2),
                             d["L0_gnn_Wm1"].rearrange("(a p) n -> p a n", p=P)).then_inc(s_wm1, 16)

                def chunk(t, i, h):
                    first = (i * 2 + h) * C * P
                    return t[bass.ds(first, C * P), :].rearrange("(c p) f -> p c f", p=P)
                for h in range(2):
                    sp.dma_start(xb[:, C * h:C * h + C, :], chunk(d["x"], 0, h)).then_inc(s_x[h], 16)
                sp.dma_start(bm1[:, :], d["L0_gnn_bm1"].partition_broadcast(P)).then_inc(s_bm1, 16)

                def body(i):
                    for h in range(2):
                        here, done = slice(C * h, C * h + C), i * 2 * C + C * h + C
                        if not past(i, 0, 2 * C):
                            nxt = chunk(d["x"], i + 1, h)
                            sp.wait_ge(s_xt_ps, done)
                            sp.dma_start(xb[:, here, :], nxt).then_inc(s_x[h], 16)
                        ra, rb = chunk(a_t, i, h), chunk(bb_t, i, h)
                        sp.wait_ge(s_a, done)
                        sp.dma_start(ra, a_s[:, here, :]).then_inc(s_ast[h], 16)
                        sp.wait_ge(s_bl, done)
                        sp.dma_start(rb, bb_s[:, here, :, :].rearrange("p c a f -> p c (a f)").bitcast(F32)).then_inc(s_bst[h], 16)
                over(sp, body, IN)
                for h in range(2):
                    sp.wait_ge(s_ast[h], 16 * IN)
                    sp.wait_ge(s_bst[h], 16 * IN)

            @block.tensor
            def _(pe):
                pe.wait_ge(s_diag, 2)
                pe.wait_ge(s_wm1, 16)

                def turn(i, b, s):
                    pe.wait_ge(s_x[s // C], i * 16 + 16)
                    at_least(pe, s_xt, b - 1)
                    pe.transpose(bank[s % 2][:, 0:P], xb[:, s, :], ident).then_inc(s_xt_ps, 1)
                turn(0, 0, 0)

                def body(i):
                    for s in range(2 * C):
                        b = i * 2 * C + s
                        if not past(i, s, 1):
                            turn(i + (s + 1) // (2 * C), b + 1, (s + 1) % (2 * C))
                        pe.wait_ge(s_xt, b + 1)
                        at_least(pe, s_a, b - 1)
                        pe.matmul(bank[2 + s % 2][:, 0:H], xt[:, s % 2, :], wm1[:, 0:H], start=True, stop=True)
                        at_least(pe, s_b, b - 1)
                        pe.matmul(bank[4 + s % 2][:, 0:H], xt[:, s % 2, :], wm1[:, H:2 * H], start=True, stop=True).then_inc(s_ab_ps, 1)
                over(pe, body, IN)

            @block.scalar
            def _(act):
                def turned(b, s):
                    at_least(act, s_ab_ps, b - 1)
                    act.wait_ge(s_xt_ps, b + 1)
                    act.copy(xt[:, s % 2, :], bank[s % 2][:, 0:P]).then_inc(s_xt, 1)

                def high(b, s):
                    act.wait_ge(s_b, b + 1)
                    act.copy(bb_s[:, s, 0, :], b_s[:, s % 2, :]).then_inc(s_bh, 1)
                turned(0, 0)

                def body(i):
                    for s in range(2 * C):
                        b = i * 2 * C + s
                        if not past(i, s, 1):
                            turned(b + 1, (s + 1) % (2 * C))
                        if s % C == 0:
                            at_least(act, s_ast[s // C], i * 16)
                        act.wait_ge(s_ab_ps, b + 1)
                        act.copy(a_s[:, s, :], bank[2 + s % 2][:, 0:H]).then_inc(s_a, 1)
                        if s % C == 1:
                            at_least(act, s_bst[s // C], i * 16)
                        if not (isinstance(b, int) and b == 0):
                            high(b - 1, (s - 1) % (2 * C))
                over(act, body, IN)
                high(NB - 1, 2 * C - 1)

            @block.vector
            def _(dve):
                dve.memset(eps[:, :], EPS)
                dve.memset(cnt[:, 0:1], 0.0)
                dve.memset(end_f[:, NB:NB + 2], 0.0)
                def masks():
                    dve.wait_ge(s_edges, 6 * 16)
                    dve.tensor_copy(cur[:, :], cur_i[:, :])
                    dve.tensor_copy(prev[:, :], prev_i[:, :])
                    dve.tensor_copy(two[:, :], two_i[:, :])
                    dve.tensor_copy(first_f[:, :], tile_first[:, :])
                    dve.tensor_copy(tile_last_f[:, :], tile_last[:, :])
                    dve.tensor_copy(last[:, :], last_i[:, :])
                    dve.wait_ge(s_iota, 1)
                    dve.tensor_copy(node[:, :], node_i[:, :]).then_inc(s_cast, 1)
                    dve.wait_ge(s_cast, 1)
                    dve.tensor_tensor(keep[:, :], cur[:, :], prev[:, :], ALU.is_equal).then_inc(s_mask, 1)
                    for c in range(2):
                        dve.tensor_scalar(rel[:, T * c:T * c + T], two[:, T * c:T * c + T], two[:, T * c:T * c + 1],
                                          None, ALU.subtract).then_inc(s_rel, 1)
                    dve.wait_ge(s_mask, 1)
                    dve.tensor_scalar(pen[:, :], keep[:, :], -RESTART, RESTART, ALU.mult, ALU.add).then_inc(s_mask, 1)

                def low(b, s):
                    dve.wait_ge(s_bh, b + 1)
                    dve.tensor_tensor(bb_s[:, s, 1, :], b_s[:, s % 2, :], bb_s[:, s, 0, :].bitcast(F32),
                                      ALU.subtract).then_inc(s_bl, 1)
                dve.wait_ge(s_bm1, 16)

                def body(i):
                    for s in range(2 * C):
                        b = i * 2 * C + s
                        dve.wait_ge(s_ab_ps, b + 1)
                        at_least(dve, s_bl, b - 1)
                        dve.tensor_tensor(b_s[:, s % 2, :], bank[4 + s % 2][:, 0:H], bm1[:, :], ALU.add).then_inc(s_b, 1)
                        if s % C == 1:
                            at_least(dve, s_bst[s // C], i * 16)
                        if not (isinstance(b, int) and b == 0):
                            low(b - 1, (s - 1) % (2 * C))
                body(0)
                masks()
                with dve.Fori(1, IN - 1) as i:
                    body(i)
                body(IN - 1)
                low(NB - 1, 2 * C - 1)
                dve.tensor_scalar(in_high[:, :], node[:, 0:1], float(WIN), float(WIN), ALU.is_ge, ALU.mult).then_inc(s_span, 1)
                dve.tensor_tensor(spans[:, :], tile_last_f[:, :], first_f[:, :], ALU.subtract).then_inc(s_span, 1)
                dve.wait_ge(s_span, 2)
                dve.tensor_tensor(in_win[:, :], node[:, 0:1], in_high[:, :], ALU.subtract)
                dve.reduce_max(widest[:, :], spans[:, :], mybir.AxisListType.X).then_inc(s_span, 1)
                dve.wait_ge(s_span, 3)
                dve.tensor_copy(span[:, :], widest[:, :])
                dve.tensor_tensor(trails[:, :], node[0:1, 1:LATE + 1], first_f[:, U + AHEAD:TILES:U],
                                  ALU.subtract).then_inc(s_span, 1)
                dve.wait_ge(s_span, 4)
                dve.reduce_max(latest[:, :], trails[:, :], mybir.AxisListType.X).then_inc(s_span, 1)
                dve.wait_ge(s_span, 5)
                dve.tensor_scalar(late_f[:, :], latest[:, :], 0.0, None, ALU.max).then_inc(s_span, 1)
                dve.wait_ge(s_span, 6)
                dve.tensor_copy(late[:, :], late_f[:, :])
                dve.wait_ge(s_w, 16 * 17)
                dve.tensor_copy(wm2_hi[:, :, :], wm2[:, :, :]).then_inc(s_wm2, 1)
                dve.wait_ge(s_wm2, 1)
                dve.tensor_tensor(wm2_lo[:, :, :], wm2[:, :, :], wm2_hi[:, :, :].bitcast(F32), ALU.subtract)

        with ExitStack() as sx:
            def tmp(name, shape, dt=F32):
                return sx.enter_context(nc.sbuf_tensor(name, shape, dt))
            ia, ib = tmp("ia", [P, U, G], I32), tmp("ib", [P, U, G], I32)
            ga, gb = tmp("ga", [P, U, G, H]), tmp("gb", [P, U, G, 2 * H])
            keep, rel = tmp("keep0", [P, U, T], BF16), tmp("rel0", [P, U, T], BF16)
            win, sel = tmp("win", [P, U, H], F32R), tmp("sel", [P, 2, T], F32R)
            h1_hi, h1_lo = tmp("h1_hi", [P, 2, 2, T], F32R), tmp("h1_lo", [P, 2, 2, T], F32R)
            h1, h2 = tmp("h1", [P, 2, 2, T]), tmp("h2", [P, 2, 2, T])
            sc = tmp("sc", [P, 2, 2, T])
            rowed = tmp("rowed", [P, 2, G, H])
            hid, back = bank[2:4], bank[4:6]
            pre = [bank[0:2], bank[6:8]]
            s_idx = sem("l0_idx")
            s_g = [sem(f"l0_gather{s}") for s in range(U)]
            s_keep = [sem(f"l0_keep{s}") for s in range(U)]
            s_rel = [sem(f"l0_rel{s}") for s in range(U)]
            s_win = [sem(f"l0_win{s}") for s in range(U)]
            s_st = [sem(f"l0_store{s}") for s in range(2)]
            s_sel, s_pre, s_hi, s_lo, s_w2, s_h2 = (sem("l0_" + x) for x in "sel pre hi lo w2 h2".split())
            s_scan, s_out_ps, s_out, s_zero = sem("l0_scan"), sem("l0_out_ps"), sem("l0_out"), sem("l0_zero")
            hit, row_i = tmp("hit", [P, ROWS]), tmp("row_i", [P, P], I32)
            row_f, row_hit, row_idx = tmp("row_f", [P, P]), tmp("row_hit", [P, P]), tmp("row_idx", [P, 1], I32)
            inverse = tmp("inverse", [P, NB])
            s_coarse, s_row_idx, s_row, s_rowf, s_fine, s_cnt, s_deg_ps, s_deg = (
                sem("c_" + x) for x in "coarse row_idx row rowf fine cnt deg_ps deg".split())
            assert IT + 1 == NB
            s_h1 = s_lo

            def ends(i, s, ahead):
                return isinstance(i, int) and i * U + s + ahead >= TILES

            def either(eng, short, long):
                widest = eng.value_load(span[0:1, 0:1], min_val=0, max_val=N)
                with eng.If(widest < WIN):
                    short()
                with eng.Else():
                    long()
            block = sx.enter_context(nc.Block())

            @block.gpsimd
            def _(pool):
                def fetch_row(b):
                    pool.wait_ge(s_row_idx, b + 1)
                    at_least(pool, s_rowf, b)
                    pool.sem_inc(s_turn, 1)
                    pool.indirect_dma_start(row_i[:, :], None, d["dst_rows"], bass.IndirectOffsetOnAxis(
                        ap=row_idx[:, :], axis=0)).then_inc(s_row, 16)

                def gathers(both):
                    def body(i):
                        for s in range(U):
                            if s == 2:
                                fetch_row(i)
                            t = i * U + s
                            pool.wait_ge(s_idx, t + 1)
                            at_least(pool, s_pre, 2 * t - 2 * U + 2)
                            pool.sem_inc(s_turn, 1)
                            for j in range(G):
                                pool.indirect_dma_start(ga[:, s, j, :], None, a_t, bass.IndirectOffsetOnAxis(
                                    ap=ia[:, s, j:j + 1], axis=0)).then_inc(s_g[s], 16)
                                if both:
                                    pool.indirect_dma_start(gb[:, s, j, :], None, bb_t, bass.IndirectOffsetOnAxis(
                                        ap=ib[:, s, j:j + 1], axis=0)).then_inc(s_g[s], 16)
                    return lambda: over(pool, body, IT)
                either(pool, gathers(False), gathers(True))
                for b in range(IT, NB):
                    fetch_row(b)

            @block.sync
            def _(sp):
                def window(base, s):
                    for part in range(2):
                        sp.dma_start(win[WIN * part:WIN * part + WIN, s, :].bitcast(F32),
                                     bb_t[bass.ds(base, WIN), H * part:H * part + H]).then_inc(s_win[s], 16)

                def loads(short):
                    def run():
                        for s in range(U):
                            sp.dma_start(keep[:, s, :], keep_t[T * s:T * s + T].partition_broadcast(P)).then_inc(s_keep[s], 16)
                            if short:
                                sp.dma_start(rel[:, s, :], rel_t[T * s:T * s + T].partition_broadcast(P)).then_inc(s_rel[s], 16)
                                window(sp.value_load(tile_first[0:1, s:s + 1], min_val=0, max_val=N - 1), s)

                        def body(i):
                            for s in range(U):
                                t = i * U + s
                                if not ends(i, s, U):
                                    nxt = t + U
                                    kr = keep_t[bass.ds(nxt * T, T)].partition_broadcast(P)
                                    if short:
                                        rr = rel_t[bass.ds(nxt * T, T)].partition_broadcast(P)
                                        base = sp.value_load(tile_first[0:1, bass.ds(nxt, 1)], min_val=0, max_val=N - 1)
                                        sp.wait_ge(s_pre, 2 * t + 2)
                                        sp.dma_start(rel[:, s, :], rr).then_inc(s_rel[s], 16)
                                        window(base, s)
                                    sp.wait_ge(s_scan, 2 * t + 2)
                                    sp.dma_start(keep[:, s, :], kr).then_inc(s_keep[s], 16)
                                out = sum_t[bass.ds(t * T, T), :].rearrange("(j p) f -> p j f", p=P)
                                sp.wait_ge(s_out, 2 * t + 2)
                                sp.dma_start(out, rowed[:, s % 2, :, :]).then_inc(s_st[s % 2], 16)
                        over(sp, body, IT)
                    return run
                either(sp, loads(True), loads(False))
                for q in range(2):
                    sp.wait_ge(s_st[q], TILES // 2 * 16)

            @block.tensor
            def _(pe):
                def turned(banks, r, s, h, start, stop, part=0):
                    for j in range(G):
                        at = H * part + P * h
                        last = pe.matmul(banks[h][:, P * j:P * j + P], r[:, s, j, at:at + P], ident,
                                         is_transpose=True, start=(start and j == 0), stop=(stop and j == G - 1))
                    return last

                def pre_long(t, s):
                    q = s % 2
                    pe.wait_ge(s_g[s], (t - s) * 32 + 128)
                    for h in range(2):
                        at_least(pe, s_h1, 2 * t - 4 + h + 1)
                        turned(pre[q], ga, s, h, True, False)
                        turned(pre[q], gb, s, h, False, False)
                        turned(pre[q], gb, s, h, False, True, part=1).then_inc(s_pre, 1)

                def pre_short(t, s):
                    q = s % 2
                    pe.wait_ge(s_sel, t + 1)
                    pe.wait_ge(s_win[s], (t - s) * 8 + 32)
                    pe.wait_ge(s_g[s], (t - s) * 16 + 64)
                    for h in range(2):
                        at_least(pe, s_lo, 2 * t - 4 + h + 1)
                        pe.matmul(pre[q][h][:, :], win[:, s, P * h:P * h + P], sel[:, q, :], start=True, stop=False)
                        turned(pre[q], ga, s, h, False, True).then_inc(s_pre, 1)

                def layer2_long(t, s):
                    q = s % 2
                    pe.wait_ge(s_h1, 2 * t + 2)
                    for m in range(2):
                        at_least(pe, s_h2, 2 * t - 2 + m + 1)
                        for k in range(2):
                            last = pe.matmul(hid[m][:, :], wm2[:, k, P * m:P * m + P], h1[:, q, k, :],
                                             start=(k == 0), stop=(k == 1))
                        last.then_inc(s_w2, 1)

                def layer2_short(t, s):
                    q = s % 2
                    pe.wait_ge(s_lo, 2 * t + 2)
                    for m in range(2):
                        at_least(pe, s_h2, 2 * t - 2 + m + 1)
                        pairs = [(w, r, k) for w, r in ((wm2_hi, h1_hi), (wm2_lo, h1_hi), (wm2_hi, h1_lo)) for k in range(2)]
                        for n, (w, r, k) in enumerate(pairs):
                            last = pe.matmul(hid[m][:, :], w[:, k, P * m:P * m + P], r[:, q, k, :],
                                             start=(n == 0), stop=(n == len(pairs) - 1))
                        last.then_inc(s_w2, 1)

                def transpose_out(t, s):
                    q = s % 2
                    pe.wait_ge(s_scan, 2 * t + 2)
                    for c in range(2):
                        at_least(pe, s_out, 2 * t - 2 + c + 1)
                        for jj in range(2):
                            for h in range(2):
                                j = 2 * c + jj
                                last = pe.transpose(back[c][:, H * jj + P * h:H * jj + P * h + P],
                                                    sc[:, q, h, P * j:P * j + P], ident)
                        last.then_inc(s_out_ps, 1)

                def tiles(pre_of, layer2):
                    def run():
                        pre_of(0, 0)

                        def body(i):
                            for s in range(U):
                                t = i * U + s
                                if not ends(i, s, 1):
                                    pre_of(t + 1, (s + 1) % U)
                                layer2(t, s)
                                if not (isinstance(t, int) and t == 0):
                                    transpose_out(t - 1, (s - 1) % U)
                        over(pe, body, IT)
                        transpose_out(TILES - 1, U - 1)
                    return run
                either(pe, tiles(pre_short, layer2_short), tiles(pre_long, layer2_long))
                pe.wait_ge(s_cnt, 1)
                pe.matmul(bank[0][:, 0:NB], below, cnt[:, 1:NB + 1], start=True, stop=False)
                pe.matmul(bank[0][:, 0:NB], wrap, cnt[:, 0:NB], start=False, stop=True).then_inc(s_deg_ps, 1)

            @block.scalar
            def _(act):
                def relu1_long(t, s):
                    q = s % 2
                    at_least(act, s_w2, 2 * t - 2)
                    for h in range(2):
                        act.wait_ge(s_pre, 2 * t + h + 1)
                        act.activation(h1[:, q, h, :], pre[q][h][:, :], ACT.Relu).then_inc(s_h1, 1)

                def relu1_short(t, s):
                    q = s % 2
                    at_least(act, s_w2, 2 * t - 2)
                    for h in range(2):
                        act.wait_ge(s_pre, 2 * t + h + 1)
                        act.activation(h1_hi[:, q, h, :], pre[q][h][:, :], ACT.Relu).then_inc(s_hi, 1)

                def relu2(t, s):
                    for m in range(2):
                        act.wait_ge(s_w2, 2 * t + m + 1)
                        at_least(act, s_scan, 2 * t - 4 + m + 1)
                        act.activation(h2[:, s % 2, m, :], hid[m][:, :], ACT.Relu, bias=bm2[:, m:m + 1]).then_inc(s_h2, 1)

                def copy_out(t, s):
                    q = s % 2
                    at_least(act, s_st[q], ((t - q) // 2 * 16) if isinstance(t, int) else (t - q) * 8)
                    for c in range(2):
                        act.wait_ge(s_out_ps, 2 * t + c + 1)
                        act.copy(rowed[:, q, 2 * c:2 * c + 2, :].rearrange("p j f -> p (j f)"), back[c][:, :]).then_inc(s_out, 1)

                def tiles(relu1):
                    def run():
                        relu1(0, 0)

                        def body(i):
                            for s in range(U):
                                t = i * U + s
                                if not ends(i, s, 1):
                                    relu1(t + 1, (s + 1) % U)
                                relu2(t, s)
                                if not (isinstance(t, int) and t == 0):
                                    copy_out(t - 1, (s - 1) % U)
                        over(act, body, IT)
                        copy_out(TILES - 1, U - 1)
                    return run
                either(act, tiles(relu1_short), tiles(relu1_long))

            @block.vector
            def _(dve):
                dve.memset(sc[:, 1, :, T - 1:T], 0.0).then_inc(s_zero, 1)
                for s in range(U):
                    dve.tensor_copy(ia[:, s, :], src[:, G * s:G * s + G])
                    dve.tensor_copy(ib[:, s, :], dst[:, G * s:G * s + G]).then_inc(s_idx, 1)
                dve.wait_ge(s_zero, 1)

                def selection(i, t, s):
                    dve.wait_ge(s_rel[s], i * 16 + 16)
                    at_least(dve, s_pre, 2 * t - 2)
                    dve.tensor_scalar(sel[:, s % 2, :], rel[:, s, :], in_win[:, :], None, ALU.is_equal).then_inc(s_sel, 1)

                def low_part(t, s):
                    q = s % 2
                    for h in range(2):
                        dve.wait_ge(s_hi, 2 * t + h + 1)
                        dve.scalar_tensor_tensor(h1_lo[:, q, h, :], pre[q][h][:, :], 0.0, h1_hi[:, q, h, :].bitcast(F32),
                                                 ALU.max, ALU.subtract).then_inc(s_lo, 1)

                def scans(t, i, s):
                    q = s % 2
                    dve.wait_ge(s_keep[s], i * 16 + 16)
                    at_least(dve, s_out_ps, 2 * t - 2)
                    for h in range(2):
                        dve.wait_ge(s_h2, 2 * t + h + 1)
                        at_least(dve, s_scan, 2 * t - 2 + h + 1)
                        dve.tensor_tensor_scan(sc[:, q, h, :], keep[:, s, :], h2[:, q, h, :],
                                               sc[:, 1 - q, h, T - 1:T], ALU.mult, ALU.add).then_inc(s_scan, 1)

                def coarse(b):
                    at_least(dve, s_row_idx, b)
                    dve.tensor_scalar(hit[:, :], last[:, :], col(node, b), 0.0, ALU.is_le, ALU.add,
                                      accum_out=col(tiles_le, b)).then_inc(s_coarse, 1)
                    dve.wait_ge(s_coarse, b + 1)
                    at_least(dve, s_row, 16 * b)
                    dve.tensor_scalar(row_idx[:, :], col(tiles_le, b), 1.0, None, ALU.mult).then_inc(s_row_idx, 1)

                def fine_count(b):
                    dve.wait_ge(s_row, 16 * b + 16)
                    at_least(dve, s_fine, b)
                    dve.tensor_copy(row_f[:, :], row_i[:, :]).then_inc(s_rowf, 1)
                    dve.wait_ge(s_rowf, b + 1)
                    dve.tensor_scalar(row_hit[:, :], row_f[:, :], col(node, b), 0.0, ALU.is_le, ALU.add,
                                      accum_out=col(fine, b)).then_inc(s_fine, 1)

                def tiles(short):
                    def run():
                        if short:
                            selection(0, 0, 0)
                            selection(0, 1, 1)
                            low_part(0, 0)

                        def body(i):
                            for s in range(U):
                                t = i * U + s
                                if short and not ends(i, s, 1):
                                    low_part(t + 1, (s + 1) % U)
                                if short and not ends(i, s, 2):
                                    selection(i + (s + 2) // U, t + 2, (s + 2) % U)
                                scans(t, i, s)
                                if s == 0:
                                    coarse(i + 1)
                                if s == 1:
                                    fine_count(i)
                                if not ends(i, s, U):
                                    nxt = (i * U + U + s) * G
                                    dve.tensor_scalar(ia[:, s, :], src[:, bass.ds(nxt, G)], 1.0, None, ALU.mult)
                                    dve.tensor_scalar(ib[:, s, :], dst[:, bass.ds(nxt, G)], 1.0, None, ALU.mult).then_inc(s_idx, 1)
                        over(dve, body, IT)
                    return run
                coarse(0)
                either(dve, tiles(True), tiles(False))
                fine_count(IT)
                dve.wait_ge(s_fine, NB)
                dve.scalar_tensor_tensor(cnt[:, 1:NB + 1], tiles_le[:, :], float(P), fine[:, :],
                                         ALU.mult, ALU.add).then_inc(s_cnt, 1)
                dve.wait_ge(s_cnt, 1)
                dve.tensor_scalar(end_f[:, 0:NB], cnt[:, 1:NB + 1], 1.0, 0.0, ALU.subtract, ALU.max)
                dve.wait_ge(s_deg_ps, 1)
                dve.tensor_tensor(fine[:, :], cnt[:, 1:NB + 1], bank[0][:, 0:NB], ALU.subtract).then_inc(s_deg, 1)
                dve.wait_ge(s_deg, 1)
                dve.tensor_scalar(flag[:, :], fine[:, :], 1.0, None, ALU.min)
                dve.tensor_scalar(tiles_le[:, :], fine[:, :], 1.0, None, ALU.max).then_inc(s_deg, 1)
                dve.wait_ge(s_deg, 2)
                dve.reciprocal(inverse[:, :], tiles_le[:, :]).then_inc(s_deg, 1)
                dve.wait_ge(s_deg, 3)
                dve.tensor_tensor(rcp[:, :], inverse[:, :], flag[:, :], ALU.mult)

        with ExitStack() as sx:
            def tmp(name, shape, dt=F32):
                return sx.enter_context(nc.sbuf_tensor(name, shape, dt))
            hg = tmp("hg", [P, 2, H])
            ht = tmp("ht", [P, 2, H])
            bf = tmp("bf", [P, 2, D])
            agg = tmp("agg", [P, 2, D])
            xa, xr = tmp("xa", [P, 2, D]), tmp("xr", [P, 2, D])
            at = tmp("at", [P, 2, 2 * D])
            hn = tmp("hn", [P, 2, H])
            y1, y = tmp("y1", [P, 2, D]), tmp("y", [P, 2, D])
            st6, mv = tmp("st6", [P, 2, 6]), tmp("mv", [P, 2, 2])
            sd, rs = tmp("sd", [P, 2]), tmp("rs", [P, 2])
            z = tmp("z", [P, 2, D])
            zt, pr = tmp("zt", [P, 2, P]), tmp("pr", [P, 2, D])
            s_idx = sem("n1_idx")
            s_g = [sem(f"n1_gather{q}") for q in range(2)]
            s_xa = [sem(f"n1_xa{q}") for q in range(2)]
            s_xr = [sem(f"n1_xr{q}") for q in range(2)]
            s_zst = [sem(f"n1_zst{q}") for q in range(2)]
            s_pst = [sem(f"n1_pst{q}") for q in range(2)]
            (s_ht_ps, s_ht, s_m_ps, s_bf, s_agg, s_at_ps, s_at, s_h_ps, s_hn, s_u_ps, s_y1, s_y, s_st6, s_mv,
             s_sd, s_rs, s_z, s_zt_ps, s_zt, s_p_ps, s_p) = (sem("n1_" + x) for x in (
                 "ht_ps ht m_ps bf agg at_ps at h_ps hn u_ps y1 y st6 mv sd rs z zt_ps zt p_ps p").split())

            def loads(b, q, each=16):
                return each * ((b - q) // 2 + 1) if isinstance(b, int) else (each // 2) * (b - q) + each
            block = sx.enter_context(nc.Block())
            S = 8

            @block.gpsimd
            def _(pool):
                def step(k, u, live):
                    if live[0]:
                        pool.wait_ge(s_idx, k + 1)
                        at_least(pool, s_ht_ps, k - 1)
                        pool.sem_inc(s_turn, 1)
                        pool.indirect_dma_start(hg[:, u, :], None, sum_t, bass.IndirectOffsetOnAxis(
                            ap=idx[:, u:u + 1], axis=0)).then_inc(s_g[u], 16)
                staged(pool, step, 1)

            @block.sync
            def _(sp):
                def step(k, u, live):
                    v = 1 - u
                    if live[1]:
                        b = k - 1
                        r = rows(d["x"], b)
                        at_least(sp, s_at_ps, b - 1)
                        sp.dma_start(xa[:, v, :], r).then_inc(s_xa[v], 16)
                    if live[3]:
                        b = k - 3
                        r = rows(d["x"], b)
                        at_least(sp, s_y1, b - 1)
                        sp.dma_start(xr[:, v, :], r).then_inc(s_xr[v], 16)
                    if live[6]:
                        b = k - 6
                        r = rows(z_t, b)
                        sp.wait_ge(s_z, b + 1)
                        sp.dma_start(r, z[:, u, :]).then_inc(s_zst[u], 16)
                    if live[8]:
                        b = k - 8
                        r = rows(p_t, b)
                        sp.wait_ge(s_p, b + 1)
                        sp.dma_start(r, pr[:, u, :]).then_inc(s_pst[u], 16)
                staged(sp, step, 9)
                for q in range(2):
                    sp.wait_ge(s_zst[q], NB // 2 * 16)
                    sp.wait_ge(s_pst[q], NB // 2 * 16)

            @block.tensor
            def _(pe):
                def step(k, u, live):
                    v = 1 - u
                    if live[0]:
                        pe.wait_ge(s_g[u], loads(k, u))
                        at_least(pe, s_ht, k)
                        for h in range(2):
                            last = pe.transpose(bank[0][:, P * h:P * h + P], hg[:, u, P * h:P * h + P], ident)
                        last.then_inc(s_ht_ps, 1)
                    if live[1]:
                        b = k - 1
                        pe.wait_ge(s_ht, b + 1)
                        at_least(pe, s_agg, b)
                        for h in range(2):
                            last = pe.matmul(bank[1][:, 0:D], ht[:, v, P * h:P * h + P], wm3[:, h, :],
                                             start=(h == 0), stop=(h == 1))
                        last.then_inc(s_m_ps, 1)
                    if live[2]:
                        b = k - 2
                        pe.wait_ge(s_agg, b + 1)
                        pe.wait_ge(s_xa[u], loads(b, u))
                        at_least(pe, s_at, b)
                        pe.transpose(bank[2][:, 0:P], xa[:, u, :], ident)
                        pe.transpose(bank[2][:, P:2 * P], agg[:, u, :], ident).then_inc(s_at_ps, 1)
                    if live[3]:
                        b = k - 3
                        pe.wait_ge(s_at, b + 1)
                        at_least(pe, s_hn, 2 * b)
                        for m in range(2):
                            for h in range(2):
                                last = pe.matmul(bank[3][:, P * m:P * m + P], wn1[:, h, P * m:P * m + P],
                                                 at[:, v, P * h:P * h + P], start=(m == 0 and h == 0), stop=(m == 1 and h == 1))
                        last.then_inc(s_h_ps, 1)
                    if live[4]:
                        b = k - 4
                        pe.wait_ge(s_hn, 2 * b + 2)
                        at_least(pe, s_y, b)
                        for h in range(2):
                            last = pe.matmul(bank[4][:, 0:D], hn[:, u, P * h:P * h + P], wn2[:, h, :],
                                             start=(h == 0), stop=(h == 1))
                        last.then_inc(s_u_ps, 1)
                    if live[6]:
                        b = k - 6
                        pe.wait_ge(s_z, b + 1)
                        at_least(pe, s_zt, b)
                        pe.transpose(bank[5][:, 0:P], z[:, u, :], ident).then_inc(s_zt_ps, 1)
                    if live[7]:
                        b = k - 7
                        pe.wait_ge(s_zt, b + 1)
                        at_least(pe, s_p, b)
                        pe.matmul(bank[6][:, 0:D], zt[:, v, :], wd_s[:, 1, :], start=True, stop=True).then_inc(s_p_ps, 1)
                staged(pe, step, S)

            @block.scalar
            def _(act):
                def step(k, u, live):
                    v = 1 - u
                    if live[0]:
                        act.wait_ge(s_ht_ps, k + 1)
                        at_least(act, s_m_ps, k - 1)
                        act.copy(ht[:, u, :], bank[0][:, 0:H]).then_inc(s_ht, 1)
                        act.sem_inc(s_act_turn, 1)
                        act.copy(idx[:, u:u + 1], col(end_f, k + 2)).then_inc(s_idx, 1)
                    if live[2]:
                        b = k - 2
                        act.wait_ge(s_at_ps, b + 1)
                        at_least(act, s_h_ps, b - 1)
                        act.copy(at[:, u, :], bank[2][:, 0:2 * D]).then_inc(s_at, 1)
                    if live[3]:
                        b = k - 3
                        act.wait_ge(s_h_ps, b + 1)
                        at_least(act, s_u_ps, b - 1)
                        for m in range(2):
                            act.activation(hn[:, v, P * m:P * m + P], bank[3][:, P * m:P * m + P], ACT.Relu,
                                           bias=bn1[:, m:m + 1]).then_inc(s_hn, 1)
                    if live[5]:
                        b = k - 5
                        act.wait_ge(s_mv, b + 1)
                        at_least(act, s_rs, b - 1)
                        act.activation(sd[:, v:v + 1], mv[:, v, 1:2], ACT.Sqrt, bias=eps[:, :]).then_inc(s_sd, 1)
                    if live[6]:
                        b = k - 6
                        act.wait_ge(s_zt_ps, b + 1)
                        at_least(act, s_p_ps, b - 1)
                        act.copy(zt[:, u, :], bank[5][:, 0:P]).then_inc(s_zt, 1)
                    if live[7]:
                        b = k - 7
                        act.wait_ge(s_p_ps, b + 1)
                        at_least(act, s_pst[v], loads(b, v) - 16)
                        act.copy(pr[:, v, :], bank[6][:, 0:D]).then_inc(s_p, 1)
                for u in range(2):
                    act.copy(idx[:, u:u + 1], end_f[:, u:u + 1]).then_inc(s_idx, 1)
                staged(act, step, S)

            @block.vector
            def _(dve):
                def step(k, u, live):
                    v = 1 - u
                    if live[2]:
                        b = k - 2
                        at_least(dve, s_agg, b - 1)
                        dve.tensor_scalar(bf[:, u, :], bm3[:, :], col(flag, b), None, ALU.mult).then_inc(s_bf, 1)
                    if live[5]:
                        b = k - 5
                        dve.wait_ge(s_xr[v], loads(b, v))
                        at_least(dve, s_y, b - 1)
                        dve.scalar_tensor_tensor(y1[:, v, :], xr[:, v, :], 2.0, bn2[:, :], ALU.mult, ALU.add).then_inc(s_y1, 1)
                    if live[2]:
                        b = k - 2
                        dve.wait_ge(s_m_ps, b + 1)
                        dve.wait_ge(s_bf, b + 1)
                        at_least(dve, s_at_ps, b - 1)
                        dve.scalar_tensor_tensor(agg[:, u, :], bank[1][:, 0:D], col(rcp, b), bf[:, u, :],
                                                 ALU.mult, ALU.add).then_inc(s_agg, 1)
                    if live[5]:
                        b = k - 5
                        dve.wait_ge(s_u_ps, b + 1)
                        dve.wait_ge(s_y1, b + 1)
                        at_least(dve, s_z, b - 1)
                        dve.tensor_tensor(y[:, v, :], bank[4][:, 0:D], y1[:, v, :], ALU.add).then_inc(s_y, 1)
                    if live[6]:
                        b = k - 6
                        dve.wait_ge(s_sd, b + 1)
                        dve.reciprocal(rs[:, u:u + 1], sd[:, u:u + 1]).then_inc(s_rs, 1)
                    if live[5]:
                        b = k - 5
                        dve.wait_ge(s_y, b + 1)
                        dve.bn_stats(st6[:, v, :], y[:, v, :]).then_inc(s_st6, 1)
                    if live[6]:
                        b = k - 6
                        dve.wait_ge(s_rs, b + 1)
                        at_least(dve, s_zst[u], loads(b, u) - 16)
                        at_least(dve, s_zt_ps, b - 1)
                        dve.tensor_scalar(z[:, u, :], y[:, u, :], mv[:, u, 0:1], rs[:, u:u + 1],
                                          ALU.subtract, ALU.mult).then_inc(s_z, 1)
                    if live[5]:
                        b = k - 5
                        dve.wait_ge(s_st6, b + 1)
                        at_least(dve, s_sd, b - 1)
                        at_least(dve, s_z, b - 1)
                        dve.sem_inc(s_aggr, 1)
                        dve.bn_aggr(mv[:, v, :], st6[:, v, :]).then_inc(s_mv, 1)
                staged(dve, step, S)

        with ExitStack() as sx:
            def tmp(name, shape, dt=F32):
                return sx.enter_context(nc.sbuf_tensor(name, shape, dt))
            ia = tmp("ia1", [P, U, G], I32)
            gp = tmp("gp", [P, U, G, D])
            pen = tmp("pen1", [P, U, T], BF16)
            wt = tmp("wt", [1, U, T])
            sc = tmp("sc1", [P, 2, T])
            rowed = tmp("rowed1", [P, 2, G, D])
            s_idx = sem("l1_idx")
            s_g = [sem(f"l1_gather{s}") for s in range(U)]
            s_pen = [sem(f"l1_pen{s}") for s in range(U)]
            s_wt = [sem(f"l1_wt{s}") for s in range(U)]
            s_st = [sem(f"l1_store{s}") for s in range(2)]
            s_pre, s_scan, s_out_ps, s_out, s_zero = sem("l1_pre"), sem("l1_scan"), sem("l1_out_ps"), sem("l1_out"), sem("l1_zero")
            pre, back = bank[0:2], bank[2:4]

            mg, za = tmp("mg", [P, D]), tmp("za", [P, D])
            zt, at, hn = tmp("zt2", [P, P]), tmp("at2", [P, P]), tmp("hn2", [P, P])
            m1, m2, agg = tmp("m1", [P, D]), tmp("m2", [P, D]), tmp("agg2", [P, D])
            y1, y = tmp("y12", [P, D]), tmp("y2", [P, D])
            st6, mv = tmp("st62", [P, 6]), tmp("mv2", [P, 2])
            sd, rs = tmp("sd2", [P, 1]), tmp("rs2", [P, 1])
            o = tmp("o", [P, D])
            s_last, s_mg, s_za, s_ost = (sem("n2_" + x) for x in "last gather za ost".split())
            (s_zt_ps, s_zt, s_q_ps, s_m1, s_m2, s_agg, s_at_ps, s_at, s_h_ps, s_hn, s_u_ps, s_y1, s_y, s_st6, s_mv,
             s_sd, s_rs, s_o) = (sem("n2_" + x) for x in (
                 "zt_ps zt q_ps m1 m2 agg at_ps at h_ps hn u_ps y1 y st6 mv sd rs o").split())
            b_turn, b_q, b_h, b_u = bank[4:8]

            OLDEST = 4
            PEEL = OLDEST + 1

            def due(i, ago):
                return not isinstance(i, int) or 0 <= i - ago < NB

            def layer(eng, step):
                def iterate(count, tiles, blocks):
                    def body(i):
                        for s in range(U):
                            step(i, s, tiles, blocks)
                    for i in range(PEEL):
                        body(i)
                    with eng.Fori(PEEL, count - 1) as i:
                        body(i)
                    body(count - 1)

                def remaining(count):
                    for i in range(count, NB + OLDEST):
                        for s in range(U):
                            step(i, s, False, True)
                trail = eng.value_load(late[0:1, 0:1], min_val=0, max_val=N)
                with eng.If(trail < 1):
                    iterate(IT, True, True)
                    remaining(IT)
                with eng.Else():
                    iterate(IT, True, False)
                    iterate(NB, False, True)
                    remaining(NB)

            def final(i):
                return isinstance(i, int) and i == IT - 1
            block = sx.enter_context(nc.Block())

            @block.gpsimd
            def _(pool):
                def step(i, s, tiles, blocks):
                    t = i * U + s
                    if blocks and s == 1 and due(i, 3):
                        k = i - 3
                        stored = TILES // 2 * 16
                        if tiles:
                            stored = (k + 1) * (U // 2 * 16) + AHEAD // 2 * 16
                        elif isinstance(k, int) and k >= IT - 3:
                            stored = min(stored, (k + 1) * (U // 2 * 16) + AHEAD // 2 * 16)
                        for q in range(2):
                            pool.wait_ge(s_st[q], stored)
                        pool.wait_ge(s_last, k + 1)
                        at_least(pool, s_m1, k)
                        pool.sem_inc(s_turn, 1)
                        pool.indirect_dma_start(mg[:, :], None, max_t, bass.IndirectOffsetOnAxis(
                            ap=idx[:, 0:1], axis=0)).then_inc(s_mg, 16)
                    if tiles:
                        pool.wait_ge(s_idx, t + 1)
                        at_least(pool, s_pre, t - U + 1)
                        pool.sem_inc(s_turn, 1)
                        for j in range(G):
                            pool.indirect_dma_start(gp[:, s, j, :], None, p_t, bass.IndirectOffsetOnAxis(
                                ap=ia[:, s, j:j + 1], axis=0)).then_inc(s_g[s], 16)
                layer(pool, step)

            @block.sync
            def _(sp):
                for s in range(U):
                    sp.dma_start(pen[:, s, :], pen_t[s * T:s * T + T].partition_broadcast(P)).then_inc(s_pen[s], 16)
                    sp.dma_start(wt[:, s, :], d["edge_weight"][:, s * T:s * T + T]).then_inc(s_wt[s], 16)

                def step(i, s, tiles, blocks):
                    t = i * U + s
                    if tiles:
                        out = max_t[bass.ds(t * T, T), :].rearrange("(j p) f -> p j f", p=P)
                        sp.wait_ge(s_out, t + 1)
                        sp.dma_start(out, rowed[:, s % 2, :, :]).then_inc(s_st[s % 2], 16)
                        if not final(i):
                            nxt = t * T + U * T
                            a, w = pen_t[bass.ds(nxt, T)].partition_broadcast(P), d["edge_weight"][:, bass.ds(nxt, T)]
                            sp.wait_ge(s_scan, t + 1)
                            sp.dma_start(pen[:, s, :], a).then_inc(s_pen[s], 16)
                            sp.dma_start(wt[:, s, :], w).then_inc(s_wt[s], 16)
                    if blocks and s == 2 and due(i, 4):
                        k = i - 4
                        r = rows(d["out"], k)
                        sp.wait_ge(s_o, k + 1)
                        sp.dma_start(r, o[:, :]).then_inc(s_ost, 16)
                    if blocks and s == 3 and due(i, 1):
                        k = i - 1
                        r = rows(z_t, k)
                        at_least(sp, s_zt_ps, k)
                        at_least(sp, s_y1, k)
                        sp.dma_start(za[:, :], r).then_inc(s_za, 16)
                layer(sp, step)
                for q in range(2):
                    sp.wait_ge(s_st[q], TILES // 2 * 16)
                sp.wait_ge(s_ost, NB * 16)

            @block.tensor
            def _(pe):
                def message(t, s):
                    q = s % 2
                    at_least(pe, s_scan, t - 1)
                    pe.wait_ge(s_wt[s], (t - s) * 4 + 16)
                    pe.matmul(pre[q][:, :], ww[:, :], wt[:, s, :], start=True, stop=False)
                    pe.wait_ge(s_g[s], (t - s) * 16 + 64)
                    for j in range(G):
                        last = pe.matmul(pre[q][:, P * j:P * j + P], gp[:, s, j, :], ident, is_transpose=True,
                                         start=False, stop=(j == G - 1))
                    last.then_inc(s_pre, 1)

                def transpose_out(t, s):
                    q = s % 2
                    pe.wait_ge(s_scan, t + 1)
                    at_least(pe, s_out, t - 1)
                    for j in range(G):
                        last = pe.transpose(back[q][:, P * j:P * j + P], sc[:, q, P * j:P * j + P], ident)
                    last.then_inc(s_out_ps, 1)

                def step(i, s, tiles, blocks):
                    t = i * U + s
                    if tiles:
                        message(t, s)
                        if not (isinstance(t, int) and t == 0):
                            transpose_out(t - 1, (s - 1) % U)
                        if final(i) and s == U - 1:
                            transpose_out(t, s)
                    if blocks and s == 0 and due(i, 3):
                        k = i - 3
                        pe.wait_ge(s_zt, k + 1)
                        at_least(pe, s_m1, k)
                        pe.matmul(b_q[:, 0:D], zt[:, :], wd_s[:, 0, :], start=True, stop=True).then_inc(s_q_ps, 1)
                        at_least(pe, s_hn, k)
                        pe.matmul(b_h[:, 0:P], w1[:, 0, :], zt[:, :], start=True, stop=False).then_inc(s_q_ps, 1)
                    if blocks and s == 1 and due(i, 3):
                        k = i - 3
                        pe.wait_ge(s_agg, k + 1)
                        at_least(pe, s_zt, k + 1)
                        at_least(pe, s_at, k)
                        pe.transpose(b_turn[:, P:2 * P], agg[:, :], ident).then_inc(s_at_ps, 1)
                    if blocks and s == 2 and due(i, 3):
                        k = i - 3
                        pe.wait_ge(s_at, k + 1)
                        pe.matmul(b_h[:, 0:P], w1[:, 1, :], at[:, :], start=False, stop=True).then_inc(s_h_ps, 1)
                    if blocks and s == 2 and due(i, 2):
                        k = i - 2
                        pe.wait_ge(s_za, k * 16 + 16)
                        at_least(pe, s_at, k)
                        at_least(pe, s_zt, k)
                        pe.transpose(b_turn[:, 0:P], za[:, :], ident).then_inc(s_zt_ps, 1)
                    if blocks and s == 3 and due(i, 3):
                        k = i - 3
                        pe.wait_ge(s_hn, k + 1)
                        at_least(pe, s_y, k)
                        pe.matmul(b_u[:, 0:D], hn[:, :], w2[:, :], start=True, stop=True).then_inc(s_u_ps, 1)
                layer(pe, step)

            @block.scalar
            def _(act):
                def step(i, s, tiles, blocks):
                    t, q = i * U + s, s % 2
                    if blocks and s == 0 and due(i, 4):
                        k = i - 4
                        act.wait_ge(s_mv, k + 1)
                        at_least(act, s_rs, k)
                        act.activation(sd[:, :], mv[:, 1:2], ACT.Sqrt, bias=eps[:, :]).then_inc(s_sd, 1)
                    if blocks and s == 2 and due(i, 3):
                        k = i - 3
                        act.wait_ge(s_at_ps, k + 1)
                        at_least(act, s_h_ps, k)
                        act.copy(at[:, :], b_turn[:, P:2 * P]).then_inc(s_at, 1)
                    if blocks and s == 3 and due(i, 3):
                        k = i - 3
                        act.wait_ge(s_h_ps, k + 1)
                        at_least(act, s_u_ps, k)
                        act.activation(hn[:, :], b_h[:, 0:P], ACT.Relu, bias=b1[:, :]).then_inc(s_hn, 1)
                    if blocks and s == 3 and due(i, 2):
                        k = i - 2
                        act.wait_ge(s_zt_ps, k + 1)
                        at_least(act, s_q_ps, 2 * k)
                        act.copy(zt[:, :], b_turn[:, 0:P]).then_inc(s_zt, 1)
                    if tiles:
                        act.wait_ge(s_out_ps, t + 1)
                        at_least(act, s_st[q], ((t - q) // 2 * 16) if isinstance(t, int) else (t - q) * 8)
                        act.copy(rowed[:, q, :, :].rearrange("p j f -> p (j f)"), back[q][:, :]).then_inc(s_out, 1)
                layer(act, step)

            @block.vector
            def _(dve):
                dve.memset(sc[:, 1, T - 1:T], 0.0).then_inc(s_zero, 1)
                for s in range(U):
                    dve.tensor_copy(ia[:, s, :], src[:, G * s:G * s + G]).then_inc(s_idx, 1)
                dve.wait_ge(s_zero, 1)

                def step(i, s, tiles, blocks):
                    t, q = i * U + s, s % 2
                    if tiles:
                        dve.wait_ge(s_pen[s], i * 16 + 16)
                        at_least(dve, s_out_ps, t - 1)
                        dve.wait_ge(s_pre, t + 1)
                        at_least(dve, s_scan, t)
                        dve.tensor_tensor_scan(sc[:, q, :], pen[:, s, :], pre[q][:, :],
                                               sc[:, 1 - q, T - 1:T], ALU.add, ALU.max).then_inc(s_scan, 1)
                        if not final(i):
                            dve.tensor_scalar(ia[:, s, :], src[:, bass.ds((i * U + U + s) * G, G)], 1.0, None, ALU.mult).then_inc(s_idx, 1)
                    if blocks and s == 0 and due(i, 3):
                        k = i - 3
                        dve.wait_ge(s_mg, k * 16 + 16)
                        dve.wait_ge(s_q_ps, 2 * k + 1)
                        at_least(dve, s_m2, k)
                        dve.tensor_tensor(m1[:, :], b_q[:, 0:D], mg[:, :], ALU.add).then_inc(s_m1, 1)
                        dve.wait_ge(s_m1, k + 1)
                        at_least(dve, s_agg, k)
                        dve.tensor_tensor(m2[:, :], m1[:, :], bm[:, :], ALU.add).then_inc(s_m2, 1)
                        dve.wait_ge(s_m2, k + 1)
                        at_least(dve, s_at_ps, k)
                        dve.tensor_scalar(agg[:, :], m2[:, :], col(flag, k), None, ALU.mult).then_inc(s_agg, 1)
                    if blocks and s == 1 and due(i, 4):
                        k = i - 4
                        dve.wait_ge(s_sd, k + 1)
                        dve.reciprocal(rs[:, :], sd[:, :]).then_inc(s_rs, 1)
                        dve.wait_ge(s_rs, k + 1)
                        at_least(dve, s_ost, k * 16)
                        dve.tensor_scalar(o[:, :], y[:, :], mv[:, 0:1], rs[:, :], ALU.subtract, ALU.mult).then_inc(s_o, 1)
                    if blocks and s == 3 and due(i, 3):
                        k = i - 3
                        dve.wait_ge(s_u_ps, k + 1)
                        dve.wait_ge(s_y1, k + 1)
                        at_least(dve, s_o, k)
                        dve.tensor_tensor(y[:, :], b_u[:, 0:D], y1[:, :], ALU.add).then_inc(s_y, 1)
                        dve.wait_ge(s_y, k + 1)
                        dve.bn_stats(st6[:, :], y[:, :]).then_inc(s_st6, 1)
                        dve.wait_ge(s_st6, k + 1)
                        dve.sem_inc(s_aggr, 1)
                        dve.bn_aggr(mv[:, :], st6[:, :]).then_inc(s_mv, 1)
                    if blocks and s == 3 and due(i, 2):
                        k = i - 2
                        dve.wait_ge(s_za, k * 16 + 16)
                        at_least(dve, s_y, k)
                        dve.tensor_tensor(y1[:, :], za[:, :], b2[:, :], ALU.add).then_inc(s_y1, 1)
                    if blocks and s == 3 and due(i, 1):
                        k = i - 1
                        at_least(dve, s_mg, k * 16)
                        dve.tensor_scalar(idx[:, 0:1], col(end_f, k), 1.0, None, ALU.mult).then_inc(s_last, 1)
                layer(dve, step)


WEIGHTS = ["L0_gnn_Wm1", "L0_gnn_bm1", "L0_gnn_Wm2", "L0_gnn_bm2", "L0_gnn_Wm3", "L0_gnn_bm3", "L0_gnn_Wn1",
           "L0_gnn_bn1", "L0_gnn_Wn2", "L0_gnn_bn2", "L1_gnn_Wm", "L1_gnn_bm", "L1_gnn_W1", "L1_gnn_b1",
           "L1_gnn_W2", "L1_gnn_b2"]


def kernel(**inputs):
    import numpy as _np
    import concourse.bacc as _bacc
    from concourse import mybir as _mybir
    from concourse.bass_utils import run_bass_kernel_spmd as _run

    def padded(a, size, fill):
        out = _np.full((size,) + a.shape[1:], fill, a.dtype)
        out[:a.shape[0]] = a
        return out

    def by_partition(a):
        return _np.ascontiguousarray(padded(a, EP, 0).reshape(ROWS, P).T)

    src, dst = _np.asarray(inputs["src"]), _np.asarray(inputs["dst"])
    dst_cur = padded(dst, EP, NP)
    dst_prev = _np.full((EP,), -1, dst.dtype)
    dst_prev[1:] = dst_cur[:-1]
    arrays = {
        "x": padded(_np.asarray(inputs["x"]), NP, 0),
        "src": by_partition(src),
        "dst": by_partition(dst),
        "dst_cur": dst_cur,
        "dst_prev": dst_prev,
        "dst_last": _np.ascontiguousarray(dst_cur[P - 1::P]),
        "dst_rows": dst_cur.reshape(ROWS, P),
        "tile_first": _np.ascontiguousarray(dst_cur[::T]).reshape(1, TILES),
        "tile_last": _np.append(dst[T - 1::T], dst[-1:]).reshape(1, TILES),
        "edge_weight": padded(_np.asarray(inputs["edge_weight"]), EP, 0).reshape(1, EP),
    }
    for name in WEIGHTS:
        arrays[name] = _np.ascontiguousarray(inputs[name])
    for name in ("L0_gnn_bm2", "L0_gnn_bn1", "L1_gnn_b1"):
        arrays[name] = _np.ascontiguousarray(arrays[name].reshape(-1, P).T)
    nc = _bacc.Bacc("TRN2", target_bir_lowering=False, num_devices=1)
    d, feed = {}, {}
    for name, a in arrays.items():
        feed[f"in_{name}"] = a
        d[name] = nc.dram_tensor(f"in_{name}", a.shape, _mybir.dt.from_np(a.dtype), kind="ExternalInput").ap()
    d["out"] = nc.dram_tensor("out_rows", (NP, D), F32, kind="ExternalOutput").ap()
    program(nc, d)
    r = _run(nc, [feed], core_ids=[0])
    return r.results[0]["out_rows"][:N]
```
